# Optimizing a Trainium2 kernel written in Bass

```python
import numpy as np
import jax
import jax.numpy as jnp

def _softmax(x, axis=-1):
    return jax.nn.softmax(x, axis=axis)

def _gelu(x):
    return jax.nn.gelu(x, approximate=True)

def _silu(x):
    return jax.nn.silu(x)

def _sigmoid(x):
    return jax.nn.sigmoid(x)

def _layernorm(x, axis=-1, eps=1e-05):
    m = jnp.mean(x, axis=axis, keepdims=True)
    v = jnp.var(x, axis=axis, keepdims=True)
    return (x - m) / jnp.sqrt(v + eps)

def _scatter_add(tgt, idx, src, axis=0):
    return tgt.at[idx].add(src)

def _segment_sum(src, seg, n):
    return jax.ops.segment_sum(src, seg, n)
kernel_name = 'mk_seq_preln_d1_jaxref_r4_48d2ce'

def setup_inputs(seed: int=0):
    np.random.seed(seed)
    _w = jnp.asarray

    def _L0_attn_setup():
        import jax, jax.numpy as jnp
        import numpy as np
        B, L, D_MODEL = (4, 512, 256)
        D_INNER = 2 * D_MODEL
        D_STATE = 64
        D_CONV = 4
        DT_RANK = D_MODEL // 16

        def _mamba_block(x, ln_w, ln_b, W_in, conv_w, conv_b, W_xproj, W_dt, b_dt, A_log, D, W_out):
            residual = x
            mu = jnp.mean(x, axis=-1, keepdims=True)
            var = jnp.mean(jnp.square(x - mu), axis=-1, keepdims=True)
            xn = (x - mu) * jax.lax.rsqrt(var + 1e-05) * ln_w + ln_b
            xz = xn @ W_in
            xi, z = jnp.split(xz, 2, axis=-1)
            xc = jnp.transpose(xi, (0, 2, 1))
            xc = jax.lax.conv_general_dilated(xc, conv_w, window_strides=(1,), padding=[(D_CONV - 1, 0)], feature_group_count=D_INNER, dimension_numbers=('NCH', 'OIH', 'NCH'))
            xc = jnp.transpose(xc, (0, 2, 1)) + conv_b
            u = jax.nn.silu(xc)
            x_dbl = u @ W_xproj
            dt_r = x_dbl[..., :DT_RANK]
            Bm = x_dbl[..., DT_RANK:DT_RANK + D_STATE]
            Cm = x_dbl[..., DT_RANK + D_STATE:]
            delta = jax.nn.softplus(dt_r @ W_dt + b_dt)
            A = -jnp.exp(A_log)

            def step(h, inputs):
                d_t, B_t, C_t, u_t = inputs
                dA = jnp.exp(d_t[:, :, None] * A)
                h = h * dA + (d_t * u_t)[:, :, None] * B_t[:, None, :]
                y_t = jnp.einsum('bdn,bn->bd', h, C_t)
                return (h, y_t)
            h0 = jnp.zeros((x.shape[0], D_INNER, D_STATE), x.dtype)
            seq = (jnp.transpose(delta, (1, 0, 2)), jnp.transpose(Bm, (1, 0, 2)), jnp.transpose(Cm, (1, 0, 2)), jnp.transpose(u, (1, 0, 2)))
            _, ys = jax.lax.scan(step, h0, seq)
            y = jnp.transpose(ys, (1, 0, 2)) + u * D
            y = y * jax.nn.silu(z)
            out = y @ W_out
            return residual + out
        key = jax.random.key(seed)
        ks = jax.random.split(key, 10)
        inp = {}
        inp['x'] = jax.random.normal(ks[0], (B, L, D_MODEL), dtype=jnp.float32)
        inp['ln_w'] = jnp.ones((D_MODEL,), jnp.float32)
        inp['ln_b'] = jnp.zeros((D_MODEL,), jnp.float32)
        inp['W_in'] = jax.random.normal(ks[1], (D_MODEL, 2 * D_INNER), jnp.float32) / np.sqrt(D_MODEL)
        inp['conv_w'] = jax.random.normal(ks[2], (D_INNER, 1, D_CONV), jnp.float32) / np.sqrt(D_CONV)
        inp['conv_b'] = jax.random.normal(ks[3], (D_INNER,), jnp.float32) * 0.01
        inp['W_xproj'] = jax.random.normal(ks[4], (D_INNER, DT_RANK + 2 * D_STATE), jnp.float32) / np.sqrt(D_INNER)
        inp['W_dt'] = jax.random.normal(ks[5], (DT_RANK, D_INNER), jnp.float32) / np.sqrt(DT_RANK)
        inp['b_dt'] = jax.random.normal(ks[6], (D_INNER,), jnp.float32) * 0.1 - 4.0
        inp['A_log'] = jnp.log(jnp.broadcast_to(jnp.arange(1, D_STATE + 1, dtype=jnp.float32), (D_INNER, D_STATE)))
        inp['D'] = jnp.ones((D_INNER,), jnp.float32)
        inp['W_out'] = jax.random.normal(ks[7], (D_INNER, D_MODEL), jnp.float32) / np.sqrt(D_INNER)
        return inp
    _L0_attn_in = _L0_attn_setup()

    def _L0_ffn_setup():
        import jax, jax.numpy as jnp
        import numpy as np
        DIM = 256
        HIDDEN = 768
        SCALE = 1.0 / 127.0

        def _dequant(w_int, dtype):
            return w_int.astype(dtype) * jnp.asarray(SCALE, dtype)
        key = jax.random.key(seed)
        k_x, k_g, k_u, k_d = jax.random.split(key, 4)
        x = jax.random.normal(k_x, (4, 512, DIM), dtype=jnp.float32)
        w_gate = jax.random.randint(k_g, (HIDDEN, DIM), -127, 128, dtype=jnp.int32)
        w_up = jax.random.randint(k_u, (HIDDEN, DIM), -127, 128, dtype=jnp.int32)
        w_down = jax.random.randint(k_d, (DIM, HIDDEN), -127, 128, dtype=jnp.int32)
        return {'x': x, 'w_gate': w_gate, 'w_up': w_up, 'w_down': w_down}
    _L0_ffn_in = _L0_ffn_setup()
    _d = {'L0_attn_x': _L0_attn_in['x'], 'L0_attn_ln_w': _L0_attn_in['ln_w'], 'L0_attn_ln_b': _L0_attn_in['ln_b'], 'L0_attn_W_in': _L0_attn_in['W_in'], 'L0_attn_conv_w': _L0_attn_in['conv_w'], 'L0_attn_conv_b': _L0_attn_in['conv_b'], 'L0_attn_W_xproj': _L0_attn_in['W_xproj'], 'L0_attn_W_dt': _L0_attn_in['W_dt'], 'L0_attn_b_dt': _L0_attn_in['b_dt'], 'L0_attn_A_log': _L0_attn_in['A_log'], 'L0_attn_D': _L0_attn_in['D'], 'L0_attn_W_out': _L0_attn_in['W_out'], 'L0_ffn_w_gate': _L0_ffn_in['w_gate'], 'L0_ffn_w_up': _L0_ffn_in['w_up'], 'L0_ffn_w_down': _L0_ffn_in['w_down']}
    _x0 = _d['L0_attn_x']
    _d['L0_attn_x'] = jax.random.normal(jax.random.fold_in(jax.random.key(seed), 1), (4, 2048, 256), dtype=_x0.dtype)
    del _x0
    return _d

def reference(L0_attn_x, L0_attn_ln_w, L0_attn_ln_b, L0_attn_W_in, L0_attn_conv_w, L0_attn_conv_b, L0_attn_W_xproj, L0_attn_W_dt, L0_attn_b_dt, L0_attn_A_log, L0_attn_D, L0_attn_W_out, L0_ffn_w_gate, L0_ffn_w_up, L0_ffn_w_down):

    def _L0_attn_ref(x, ln_w, ln_b, W_in, conv_w, conv_b, W_xproj, W_dt, b_dt, A_log, D, W_out):
        import jax, jax.numpy as jnp
        import numpy as np
        B, L, D_MODEL = (4, 512, 256)
        D_INNER = 2 * D_MODEL
        D_STATE = 64
        D_CONV = 4
        DT_RANK = D_MODEL // 16

        def _mamba_block(x, ln_w, ln_b, W_in, conv_w, conv_b, W_xproj, W_dt, b_dt, A_log, D, W_out):
            residual = x
            mu = jnp.mean(x, axis=-1, keepdims=True)
            var = jnp.mean(jnp.square(x - mu), axis=-1, keepdims=True)
            xn = (x - mu) * jax.lax.rsqrt(var + 1e-05) * ln_w + ln_b
            xz = xn @ W_in
            xi, z = jnp.split(xz, 2, axis=-1)
            xc = jnp.transpose(xi, (0, 2, 1))
            xc = jax.lax.conv_general_dilated(xc, conv_w, window_strides=(1,), padding=[(D_CONV - 1, 0)], feature_group_count=D_INNER, dimension_numbers=('NCH', 'OIH', 'NCH'))
            xc = jnp.transpose(xc, (0, 2, 1)) + conv_b
            u = jax.nn.silu(xc)
            x_dbl = u @ W_xproj
            dt_r = x_dbl[..., :DT_RANK]
            Bm = x_dbl[..., DT_RANK:DT_RANK + D_STATE]
            Cm = x_dbl[..., DT_RANK + D_STATE:]
            delta = jax.nn.softplus(dt_r @ W_dt + b_dt)
            A = -jnp.exp(A_log)

            def step(h, inputs):
                d_t, B_t, C_t, u_t = inputs
                dA = jnp.exp(d_t[:, :, None] * A)
                h = h * dA + (d_t * u_t)[:, :, None] * B_t[:, None, :]
                y_t = jnp.einsum('bdn,bn->bd', h, C_t)
                return (h, y_t)
            h0 = jnp.zeros((x.shape[0], D_INNER, D_STATE), x.dtype)
            seq = (jnp.transpose(delta, (1, 0, 2)), jnp.transpose(Bm, (1, 0, 2)), jnp.transpose(Cm, (1, 0, 2)), jnp.transpose(u, (1, 0, 2)))
            _, ys = jax.lax.scan(step, h0, seq)
            y = jnp.transpose(ys, (1, 0, 2)) + u * D
            y = y * jax.nn.silu(z)
            out = y @ W_out
            return residual + out
        return _mamba_block(x, ln_w, ln_b, W_in, conv_w, conv_b, W_xproj, W_dt, b_dt, A_log, D, W_out)

    def _L0_ffn_ref(x, w_gate, w_up, w_down):
        import jax, jax.numpy as jnp
        import numpy as np
        DIM = 256
        HIDDEN = 768
        SCALE = 1.0 / 127.0

        def _dequant(w_int, dtype):
            return w_int.astype(dtype) * jnp.asarray(SCALE, dtype)
        wg = _dequant(w_gate, x.dtype)
        wu = _dequant(w_up, x.dtype)
        wd = _dequant(w_down, x.dtype)
        gate = jnp.einsum('bsd,hd->bsh', x, wg)
        up = jnp.einsum('bsd,hd->bsh', x, wu)
        h = jax.nn.silu(gate) * up
        return jnp.einsum('bsh,dh->bsd', h, wd)
    x = L0_attn_x
    x = x + _L0_attn_ref(_layernorm(x, axis=-1), L0_attn_ln_w, L0_attn_ln_b, L0_attn_W_in, L0_attn_conv_w, L0_attn_conv_b, L0_attn_W_xproj, L0_attn_W_dt, L0_attn_b_dt, L0_attn_A_log, L0_attn_D, L0_attn_W_out)
    x = x + _L0_ffn_ref(_layernorm(x, axis=-1), L0_ffn_w_gate, L0_ffn_w_up, L0_ffn_w_down)
    return x

_drawn_inputs = setup_inputs


def setup_inputs(seed=0):
    import zlib

    import numpy as np

    out = dict(_drawn_inputs(seed))
    spreads = {'L0_attn_ln_w': (1.0, 0.2), 'L0_attn_ln_b': (0.0, 0.1), 'L0_attn_D': (1.0, 0.2)}
    factors = {'L0_attn_conv_b': 21.421,
     'L0_attn_b_dt': 200.0,
     'L0_attn_W_xproj': 8.0,
     'L0_attn_W_dt': 8.0,
     'L0_attn_A_log': 8.0}
    for name, (base, spread) in spreads.items():
        noise = np.random.default_rng([zlib.crc32(name.encode()), seed]).standard_normal(out[name].shape)
        drawn = base * np.exp(spread * noise) if base else spread * noise
        out[name] = jnp.asarray(drawn.astype(out[name].dtype))
    for name, factor in factors.items():
        out[name] = (out[name] * factor).astype(out[name].dtype)
    return out
```

```python
from contextlib import ExitStack

import concourse.bass as bass
from concourse import mybir

ALU = mybir.AluOpType
ACT = mybir.ActivationFunctionType
F32 = mybir.dt.float32
BF16 = mybir.dt.bfloat16
I32 = mybir.dt.int32

P = 128
BATCH, SEQ, DM = 4, 2048, 256
DI, NS, RANK, TAPS = 512, 64, 16, 4
HID = 768
TOK = BATCH * SEQ
EPS = 1e-5
WSCALE = 1.0 / 127.0

TW = 512
NT = TOK // TW
TPB = SEQ // TW
SUB = TW // P
KD = DM // P
MI = DI // P
MH = HID // P

CH = 256
NB = TOK // CH
CPB = SEQ // CH
NG = DI // P
PAIRS = P // 2
QUADS = PAIRS // 4
SEG = CH + 1
COMBOS = [(i, j) for j in range(3) for i in range(3) if i + j < 4]
WIN = 8
SETS = CH // 16
ACT_QUADS = [q for q in range(QUADS) if q % 8 not in (2, 5, 7)]
LAG = 2
FIRST_C = 3


def norm_stage(nc, d, xnT):
    with ExitStack() as ctx:
        def sb(name, shape, dt=F32):
            return ctx.enter_context(nc.sbuf_tensor(name, shape, dt))

        def sem(name):
            return ctx.enter_context(nc.semaphore(name))

        x = sb("n_x", [P, 2, SUB, DM])
        xa = sb("n_xa", [P, 2, SUB, DM])
        xn = sb("n_xn", [P, 2, SUB, DM])
        res = sb("n_res", [P, 2, SUB, DM])
        stats = sb("n_stats", [P, 2, 2, SUB, 6])
        mv = sb("n_mv", [P, 2, 2, SUB, 2])
        veps = sb("n_veps", [P, 2, 2, SUB])
        rstd = sb("n_rstd", [P, 2, 2, SUB])
        half = sb("n_half", [P, SUB])
        spare = sb("n_spare", [P, 1])
        ident = sb("n_ident", [P, P])
        lnw = sb("n_lnw", [P, KD])
        lnb = sb("n_lnb", [P, KD])
        tr = ctx.enter_context(nc.psum_tensor("n_tr", [P, 2, KD, TW], F32))

        x_loaded = [sem("x_loaded0"), sem("x_loaded1")]
        par_loaded = sem("par_loaded")
        consts = sem("consts")
        stats_done = sem("stats_done")
        mv_done = sem("mv_done")
        veps_done = sem("veps_done")
        rstd_done = sem("rstd_done")
        xa_done = sem("xa_done")
        xn_done = sem("xn_done")
        res_done = sem("res_done")
        res_stored = [sem("res_stored0"), sem("res_stored1")]
        tr_done = sem("tr_done")
        tr_read = sem("tr_read")

        block = ctx.enter_context(nc.Block())
        xv = d["x"].rearrange("(i s p) c -> i p s c", s=SUB, p=P)
        rv = d["res"].rearrange("(i s p) c -> i p s c", s=SUB, p=P)

        @block.sync
        def _(sp):
            sp.dma_start(lnw[:, :], d["ln_w"].rearrange("(k p) -> p k", p=P), allow_slow_non_contiguous=True).then_inc(par_loaded, 16)
            sp.dma_start(lnb[:, :], d["ln_b"].rearrange("(k p) -> p k", p=P), allow_slow_non_contiguous=True).then_inc(par_loaded, 16)
            with sp.Fori(0, NT // 2) as j:
                for s in range(2):
                    sp.wait_ge(res_done, j * 2 + s + 1)
                    sp.dma_start(x[:, s], xv[j * 2 + s]).then_inc(x_loaded[s], 16)

        @block.vector
        def _(dve):
            def layernorm(j, s, k, src, dst, done):
                i = j * 2 + s
                for g in range(SUB):
                    nc.vector.bn_stats(stats[:, s, k, g, :], src[:, s, g, :]).then_inc(stats_done, 1)
                n = j * 16 + k * 8 + s * 4
                dve.wait_ge(stats_done, n + 4)
                nc.vector.memset(spare[:, 0:1], 0.0)
                for g in range(SUB):
                    nc.vector.bn_aggr(mv[:, s, k, g, :], stats[:, s, k, g, :]).then_inc(mv_done, 1)
                dve.wait_ge(mv_done, n + 4)
                nc.vector.tensor_scalar(veps[:, s, k, :], mv[:, s, k, :, 1], EPS, None, ALU.add).then_inc(veps_done, 1)

            def scaled(j, s, k, src, dst, done):
                dve.wait_ge(rstd_done, j * 4 + k * 2 + s + 1)
                for g in range(SUB):
                    nc.vector.tensor_scalar(dst[:, s, g, :], src[:, s, g, :], mv[:, s, k, g, 0:1],
                                            rstd[:, s, k, g:g + 1], ALU.subtract, ALU.mult).then_inc(done, 1)

            with dve.Fori(0, NT // 2) as j:
                for s in range(2):
                    dve.wait_ge(x_loaded[s], j * 16 + 16)
                    layernorm(j, s, 0, x, xa, xa_done)
                for s in range(2):
                    dve.wait_ge(res_done, j * 2 + s + 1)
                    scaled(j, s, 0, x, xa, xa_done)
                for s in range(2):
                    dve.wait_ge(xa_done, j * 8 + s * 4 + 4)
                    layernorm(j, s, 1, xa, xn, xn_done)
                for s in range(2):
                    dve.wait_ge(tr_done, j * 2 + s + 1)
                    scaled(j, s, 1, xa, xn, xn_done)

        @block.gpsimd
        def _(pool):
            nc.gpsimd.memset(half[:, :], -0.5).then_inc(consts, 1)
            nc.gpsimd.memset(ident[:, :], 0.0).then_inc(consts, 1)
            pool.wait_ge(consts, 2)
            nc.gpsimd.affine_select(out=ident[:, :], in_=ident[:, :], compare_op=ALU.not_equal, fill=1.0, base=0,
                                    pattern=[[-1, P]], channel_multiplier=1).then_inc(consts, 1)
            pool.sem_inc(res_done, 2)
            with pool.Fori(0, NT // 2) as j:
                for k in range(2):
                    for s in range(2):
                        pool.wait_ge(veps_done, j * 4 + k * 2 + s + 1)
                        nc.gpsimd.tensor_tensor(rstd[:, s, k, :], veps[:, s, k, :], half[:, :],
                                                ALU.pow).then_inc(rstd_done, 1)
                for s in range(2):
                    pool.wait_ge(xn_done, j * 8 + s * 4 + 4)
                    pool.wait_ge(res_stored[s], j * 16 + 16)
                    nc.gpsimd.tensor_tensor(res[:, s], x[:, s], xa[:, s], ALU.add).then_inc(res_done, 1)

        @block.tensor
        def _(pe):
            pe.wait_ge(consts, 3)
            pe.sem_inc(tr_done, 2)
            with pe.Fori(0, NT // 2) as j:
                for s in range(2):
                    pe.wait_ge(xn_done, j * 8 + s * 4 + 4)
                    pe.wait_ge(tr_read, j * 4 + s * 2 + 2)
                    for k in range(KD):
                        for g in range(SUB):
                            last = nc.tensor.transpose(tr[:, s, k, g * P:(g + 1) * P],
                                                       xn[:, s, g, k * P:(k + 1) * P], ident[:, :])
                    last.then_inc(tr_done, 1)

        @block.scalar
        def _(act):
            act.sem_inc(tr_read, 4)
            act.sem_inc(res_stored[0], 16)
            act.sem_inc(res_stored[1], 16)
            act.wait_ge(par_loaded, 32)
            with act.Fori(0, NT // 2) as j:
                for s in range(2):
                    act.wait_ge(tr_done, j * 2 + s + 3)
                    for k in range(KD):
                        nc.scalar.activation(xnT[:, k, bass.ds((j * 2 + s) * TW, TW)], tr[:, s, k, :], ACT.Identity,
                                             bias=lnb[:, k:k + 1], scale=lnw[:, k:k + 1]).then_inc(tr_read, 1)
                    act.wait_ge(res_done, j * 2 + s + 3)
                    act.dma_start(rv[j * 2 + s], res[:, s]).then_inc(res_stored[s], 16)
            for s in range(2):
                act.wait_ge(res_stored[s], 16 * (NT // 2 + 1))


def decay_stage(nc, d):
    with ExitStack() as ctx:
        def sb(name, shape, dt=F32):
            return ctx.enter_context(nc.sbuf_tensor(name, shape, dt))

        def sem(name):
            return ctx.enter_context(nc.semaphore(name))

        a = sb("d_a", [P, MI, NS])
        parts = sb("d_parts", [P, 3, MI, NS], BF16)
        zeros = sb("d_zeros", [P, PAIRS * P // 2])
        a_loaded = sem("a_loaded")
        a_exp = sem("a_exp")
        a_step = sem("a_step")
        zeroed = sem("zeroed")
        image_zero = sem("image_zero")
        parts_stored = sem("parts_stored")
        placed = sem("placed")
        block = ctx.enter_context(nc.Block())

        @block.gpsimd
        def _(pool):
            nc.gpsimd.memset(zeros[:, :], 0.0).then_inc(zeroed, 1)

        @block.scalar
        def _(act):
            act.wait_ge(a_loaded, 16)
            nc.scalar.activation(a[:, :, :], a[:, :, :], ACT.Exp).then_inc(a_exp, 1)

        @block.vector
        def _(dve):
            count = [0]

            def step(ins):
                count[0] += 1
                ins.then_inc(a_step, 1)
                dve.wait_ge(a_step, count[0])

            dve.wait_ge(a_exp, 1)
            step(nc.vector.tensor_scalar(a[:, :, :], a[:, :, :], -1.0, -3.0e38, ALU.mult, ALU.max))
            step(nc.vector.tensor_copy(parts[:, 0], a[:, :, :]))
            step(nc.vector.tensor_tensor(a[:, :, :], a[:, :, :], parts[:, 0], ALU.subtract))
            step(nc.vector.tensor_copy(parts[:, 1], a[:, :, :]))
            step(nc.vector.tensor_tensor(parts[:, 2], a[:, :, :], parts[:, 1], ALU.subtract))

        @block.sync
        def _(sp):
            sp.dma_start(a[:, :, :], d["A_log"].rearrange("(m p) n -> p m n", p=P)).then_inc(a_loaded, 16)
            sp.wait_ge(zeroed, 1)
            for g in range(NG):
                sp.dma_start(d["a_image"][g], zeros[:, :].bitcast(BF16)).then_inc(image_zero, 16)
            sp.wait_ge(a_step, 5)
            for k in range(3):
                sp.dma_start(d["a_parts"][k].rearrange("(m p) n -> p m n", p=P),
                             parts[:, k]).then_inc(parts_stored, 16)
            sp.wait_ge(parts_stored, 48)
            sp.wait_ge(image_zero, 16 * NG)
            row = PAIRS * P
            image = d["a_image"].tensor
            for g in range(NG):
                for c, (i, _) in enumerate(COMBOS):
                    for h in range(2):
                        dst = bass.AP(image, (g * P + c * 16 + 8 * h) * row + NS * h,
                                      [[row + 8 * P, 8], [P, 8], [1, NS]])
                        src = d["a_parts"][i, g * P + 64 * h:g * P + 64 * h + 64, :].rearrange("(k s) n -> k s n", k=8)
                        sp.dma_start(dst, src).then_inc(placed, 16)
            sp.wait_ge(placed, 16 * NG * len(COMBOS) * 2)


def project_stage(nc, d, xnT):
    with ExitStack() as ctx:
        def sb(name, shape, dt=F32):
            return ctx.enter_context(nc.sbuf_tensor(name, shape, dt))

        def sem(name):
            return ctx.enter_context(nc.semaphore(name))

        w_in = sb("p_w_in", [P, KD, 2 * DI])
        w_x = sb("p_w_x", [P, MI, RANK + 4 * NS])
        w_dt = sb("p_w_dt", [RANK, DI])
        conv_w = sb("p_conv_w", [P, MI, TAPS])
        conv_b = sb("p_conv_b", [P, MI])
        b_dt = sb("p_b_dt", [P, MI])
        xi = sb("p_xi", [P, MI, TAPS - 1 + TW])
        acc = sb("p_acc", [P, MI, TW])
        u = sb("p_u", [P, 2, MI, TW])
        sz = sb("p_sz", [P, MI, TW])
        dtr = sb("p_dtr", [RANK, TW])
        bc = sb("p_bc", [P, 2, TW])
        v = sb("p_v", [P, MI, TW])
        ex = sb("p_ex", [P, MI, TW])
        w1 = sb("p_w1", [P, MI, TW])
        lw = sb("p_lw", [P, MI, TW])
        du = sb("p_du", [P, MI, TW])
        dparts = sb("p_dparts", [P, 3, MI, TW], BF16)
        uparts = sb("p_uparts", [P, 3, MI, TW], BF16)
        in_bank = ctx.enter_context(nc.psum_tensor("p_in", [P, 4, TW], F32))
        bk_bank = ctx.enter_context(nc.psum_tensor("p_bk", [P, 4, TW], F32))

        weights = sem("weights")
        in_ready = sem("in_ready")
        in_read = sem("in_read")
        xi_free = sem("xi_free")
        conv_step = sem("conv_step")
        conv_done = sem("conv_done")
        u_ready = sem("u_ready")
        back_ready = sem("back_ready")
        back_read = sem("back_read")
        abs_done = sem("abs_done")
        exp_done = sem("exp_done")
        w1_done = sem("w1_done")
        ln_done = sem("ln_done")
        tail_done = sem("tail_done")
        log_done = sem("log_done")
        delta_done = sem("delta_done")
        du_done = sem("du_done")
        d1_done, dr_done, d2_done, d3_done = sem("d1_done"), sem("dr_done"), sem("d2_done"), sem("d3_done")
        u1_done, ur_done, u2_done = sem("u1_done"), sem("ur_done"), sem("u2_done")
        u3_done = sem("u3_done")
        u_stored = [sem("u_stored0"), sem("u_stored1")]
        sz_stored = sem("sz_stored")
        bc_stored = sem("bc_stored")
        dparts_stored = sem("dparts_stored")
        uparts_stored = sem("uparts_stored")
        n_weights = 10

        block = ctx.enter_context(nc.Block())

        def over_tiles(eng, front, middle, back):
            front(0, 0, 0)
            middle(0, 0, 0)

            def batch(b, last):
                for c in range(TPB):
                    nb, nc_ = (b, c + 1) if c + 1 < TPB else (b + 1, 0)
                    more = not (last and c + 1 == TPB)
                    if more:
                        front(nb * TPB + nc_, nc_, nb)
                    back(b * TPB + c, c, b)
                    if more:
                        middle(nb * TPB + nc_, nc_, nb)

            with eng.Fori(0, BATCH - 1) as b:
                batch(b, False)
            batch(BATCH - 1, True)

        def nothing(i, c, b):
            pass

        @block.sync
        def _(sp):
            wx = d["W_xproj"].rearrange("(m p) n -> p m n", p=P)
            sp.dma_start(w_in[:, :, :], d["W_in"].rearrange("(k p) n -> p k n", p=P)).then_inc(weights, 16)
            sp.dma_start(w_x[:, :, 0:RANK], wx[:, :, 0:RANK]).then_inc(weights, 16)
            for r in range(4):
                at, frm = RANK + NS * r, RANK + NS * (r // 2)
                sp.dma_start(w_x[:, :, at:at + NS], wx[:, :, frm:frm + NS]).then_inc(weights, 16)
            sp.dma_start(w_dt[:, :], d["W_dt"]).then_inc(weights, 16)
            sp.dma_start(conv_w[:, :, :], d["conv_w"].rearrange("(m p) o k -> p m (o k)", p=P)).then_inc(weights, 16)
            sp.dma_start(conv_b[:, :], d["conv_b"].rearrange("(m p) -> p m", p=P), allow_slow_non_contiguous=True).then_inc(weights, 16)
            sp.dma_start(b_dt[:, :], d["b_dt"].rearrange("(m p) -> p m", p=P), allow_slow_non_contiguous=True).then_inc(weights, 16)

            def tile_of(dram, i):
                return dram.rearrange("(m p) t -> p m t", p=P)[:, :, bass.ds(i * TW, TW)]

            def front_stores(i, c, b):
                sp.wait_ge(in_read, i * 8 + 12)
                sp.dma_start(tile_of(d["sz"], i), sz[:, :, :]).then_inc(sz_stored, 16)
                sp.wait_ge(u_ready, i * 4 + 8)
                sp.dma_start(tile_of(d["u"], i), u[:, c % 2]).then_inc(u_stored[c % 2], 16)

            def back_stores(i, c, b):
                sp.wait_ge(back_read, i * 7 + 10)
                sp.dma_start(d["B"][:, bass.ds(i * TW, TW)], bc[:, 0, :]).then_inc(bc_stored, 16)
                sp.wait_ge(d3_done, i + 1)
                sp.dma_start(d["C"][:, bass.ds(i * TW, TW)], bc[:, 1, :]).then_inc(bc_stored, 16)
                for k in range(3):
                    sp.dma_start(tile_of(d["dparts"][k], i), dparts[:, k]).then_inc(dparts_stored, 16)
                sp.wait_ge(u3_done, i + 2)
                for k in range(3):
                    sp.dma_start(tile_of(d["uparts"][k], i), uparts[:, k]).then_inc(uparts_stored, 16)

            over_tiles(sp, nothing, front_stores, back_stores)
            for s in range(2):
                sp.wait_ge(u_stored[s], 16 * (NT // 2 + 1))
            sp.wait_ge(sz_stored, 16 * (NT + 1))
            sp.wait_ge(bc_stored, 32 * (NT + 1))
            sp.wait_ge(dparts_stored, 48 * (NT + 1))
            sp.wait_ge(uparts_stored, 48 * (NT + 1))

        @block.tensor
        def _(pe):
            pe.wait_ge(weights, 16 * n_weights)

            def front(i, c, b):
                for m in range(2 * MI):
                    pe.wait_ge(in_read, i * 8 + m + 1)
                    for k in range(KD):
                        last = nc.tensor.matmul(in_bank[:, m % 4, :], w_in[:, k, m * P:(m + 1) * P],
                                                xnT[:, k, bass.ds(i * TW, TW)], start=(k == 0), stop=(k == KD - 1))
                    last.then_inc(in_ready, 1)

            def back(i, c, b):
                pe.wait_ge(u_ready, i * 4 + 8)
                pe.wait_ge(back_read, i * 7 + 7)
                for bank, lo, n in ((2, 0, RANK), (0, RANK, 2 * NS), (1, RANK + 2 * NS, 2 * NS)):
                    for m in range(MI):
                        last = nc.tensor.matmul(bk_bank[0:n, bank, :], w_x[:, m, lo:lo + n], u[:, c % 2, m, :],
                                                start=(m == 0), stop=(m == MI - 1))
                    last.then_inc(back_ready, 1)
                for m in range(MI):
                    pe.wait_ge(back_read, i * 7 + (8, 8, 11, 12)[m])
                    nc.tensor.matmul(bk_bank[:, (3, 2)[m % 2], :], w_dt[:, m * P:(m + 1) * P], dtr[:, :],
                                     start=True, stop=True).then_inc(back_ready, 1)

            over_tiles(pe, front, nothing, back)

        @block.scalar
        def _(act):
            act.sem_inc(in_read, 4)
            act.sem_inc(back_read, 7)
            act.sem_inc(u_ready, 4)
            act.sem_inc(u_stored[0], 16)
            act.sem_inc(u_stored[1], 16)
            act.sem_inc(sz_stored, 16)
            act.sem_inc(bc_stored, 32)
            act.sem_inc(dparts_stored, 48)
            act.sem_inc(uparts_stored, 48)
            act.wait_ge(weights, 16 * n_weights)

            def front(i, c, b):
                act.wait_ge(xi_free, i + 1)
                for m in range(MI):
                    act.wait_ge(in_ready, i * 8 + m + 1)
                    nc.scalar.activation(xi[:, m, TAPS - 1:TAPS - 1 + TW], in_bank[:, m, :],
                                         ACT.Identity).then_inc(in_read, 1)
                act.wait_ge(sz_stored, i * 16 + 16)
                for m in range(MI):
                    act.wait_ge(in_ready, i * 8 + MI + m + 1)
                    nc.scalar.activation(sz[:, m, :], in_bank[:, m, :], ACT.Silu).then_inc(in_read, 1)

            def middle(i, c, b):
                act.wait_ge(u_stored[c % 2], b * 32 + (c // 2) * 16 + 16)
                for m in range(MI):
                    act.wait_ge(conv_done, i * 4 + m + 1)
                    nc.scalar.activation(u[:, c % 2, m, :], acc[:, m, :], ACT.Silu,
                                         bias=conv_b[:, m:m + 1]).then_inc(u_ready, 1)

            def back(i, c, b):
                act.wait_ge(back_ready, i * 7 + 1)
                nc.scalar.activation(dtr[:, :], bk_bank[0:RANK, 2, :], ACT.Identity).then_inc(back_read, 1)
                act.wait_ge(bc_stored, i * 32 + 32)
                for k in range(2):
                    act.wait_ge(back_ready, i * 7 + 2 + k)
                    nc.scalar.activation(bc[:, k, :], bk_bank[:, k, :], ACT.Identity).then_inc(back_read, 1)
                act.wait_ge(delta_done, i + 1)
                for m in range(MI):
                    act.wait_ge(back_ready, i * 7 + 4 + m)
                    nc.scalar.activation(v[:, m, :], bk_bank[:, (3, 2)[m % 2], :], ACT.Identity,
                                         bias=b_dt[:, m:m + 1]).then_inc(back_read, 1)
                act.wait_ge(back_read, i * 7 + 14)
                act.wait_ge(u3_done, i + 1)
                nc.scalar.activation(ex[:, :, :], v[:, :, :], ACT.Abs).then_inc(abs_done, 1)
                act.wait_ge(abs_done, i + 1)
                nc.scalar.activation(ex[:, :, :], ex[:, :, :], ACT.Exp, scale=-1.0).then_inc(exp_done, 1)
                act.wait_ge(w1_done, i + 1)
                nc.scalar.activation(lw[:, :, :], w1[:, :, :], ACT.Ln).then_inc(ln_done, 1)

            over_tiles(act, front, middle, back)

        @block.vector
        def _(dve):
            dve.sem_inc(delta_done, 1)
            nc.vector.memset(xi[:, :, 0:TAPS - 1], 0.0).then_inc(xi_free, 1)
            dve.wait_ge(weights, 16 * n_weights)

            def front(i, c, b):
                dve.wait_ge(xi_free, i + 1)
                for k in range(TAPS):
                    for m in range(MI):
                        tap, wk = xi[:, m, k:k + TW], conv_w[:, m, k:k + 1]
                        if k == 0:
                            dve.wait_ge(in_read, i * 8 + 5 + m)
                            dve.wait_ge(u_ready, i * 4 + m + 1)
                            nc.vector.tensor_scalar(acc[:, m, :], tap, wk, None, ALU.mult).then_inc(conv_step, 1)
                        else:
                            dve.wait_ge(conv_step, i * 12 + (k - 1) * 4 + m + 1)
                            nc.vector.scalar_tensor_tensor(
                                out=acc[:, m, :], in0=tap, scalar=wk, in1=acc[:, m, :], op0=ALU.mult,
                                op1=ALU.add).then_inc(conv_step if k < TAPS - 1 else conv_done, 1)
                dve.wait_ge(conv_done, i * 4 + 4)
                if c + 1 < TPB:
                    nc.vector.tensor_copy(xi[:, :, 0:TAPS - 1], xi[:, :, TW:TW + TAPS - 1]).then_inc(xi_free, 1)
                else:
                    nc.vector.memset(xi[:, :, 0:TAPS - 1], 0.0).then_inc(xi_free, 1)

            def back(i, c, b):
                dve.wait_ge(exp_done, i + 1)
                nc.vector.tensor_scalar(w1[:, :, :], ex[:, :, :], 1.0, None, ALU.add).then_inc(w1_done, 1)
                dve.wait_ge(w1_done, i + 1)
                nc.vector.scalar_tensor_tensor(out=ex[:, :, :], in0=w1[:, :, :], scalar=1.0, in1=ex[:, :, :],
                                               op0=ALU.subtract, op1=ALU.subtract).then_inc(tail_done, 1)
                dve.wait_ge(tail_done, i + 1)
                dve.wait_ge(ln_done, i + 1)
                nc.vector.tensor_tensor(lw[:, :, :], lw[:, :, :], ex[:, :, :], ALU.subtract).then_inc(log_done, 1)
                dve.wait_ge(log_done, i + 1)
                nc.vector.scalar_tensor_tensor(out=lw[:, :, :], in0=v[:, :, :], scalar=0.0, in1=lw[:, :, :],
                                               op0=ALU.max, op1=ALU.add).then_inc(delta_done, 1)
                for src, rest, parts, stored, first, whole, one, left, two in (
                        (lw, w1, dparts, dparts_stored, delta_done, i + 2, d1_done, dr_done, d2_done),
                        (du, ex, uparts, uparts_stored, du_done, i + 1, u1_done, ur_done, u2_done)):
                    dve.wait_ge(first, whole)
                    dve.wait_ge(stored, i * 48 + 48)
                    nc.vector.tensor_copy(parts[:, 0], src[:, :, :]).then_inc(one, 1)
                    dve.wait_ge(one, i + 1)
                    nc.vector.tensor_tensor(rest[:, :, :], src[:, :, :], parts[:, 0], ALU.subtract).then_inc(left, 1)
                    dve.wait_ge(left, i + 1)
                    nc.vector.tensor_copy(parts[:, 1], rest[:, :, :]).then_inc(two, 1)

            over_tiles(dve, front, nothing, back)

        @block.gpsimd
        def _(pool):
            pool.sem_inc(u3_done, 1)

            def back(i, c, b):
                pool.wait_ge(delta_done, i + 2)
                nc.gpsimd.tensor_tensor(du[:, :, :], lw[:, :, :], u[:, c % 2], ALU.mult).then_inc(du_done, 1)
                pool.wait_ge(d2_done, i + 1)
                nc.gpsimd.tensor_tensor(dparts[:, 2], w1[:, :, :], dparts[:, 1], ALU.subtract).then_inc(d3_done, 1)
                pool.wait_ge(u2_done, i + 1)
                nc.gpsimd.tensor_tensor(uparts[:, 2], ex[:, :, :], uparts[:, 1], ALU.subtract).then_inc(u3_done, 1)

            over_tiles(pool, nothing, nothing, back)


def scan_stage(nc, d):
    with ExitStack() as ctx:
        def sb(name, shape, dt=F32):
            return ctx.enter_context(nc.sbuf_tensor(name, shape, dt))

        def sem(name):
            return ctx.enter_context(nc.semaphore(name))

        NA = len(ACT_QUADS)
        ND = QUADS - NA
        act_before = [sum(r in ACT_QUADS for r in range(q)) for q in range(QUADS)]
        dve_before = [q - act_before[q] for q in range(QUADS)]
        NL = len(COMBOS) + 3 + 2

        H = [sb(f"s_h{s}", [P, PAIRS, SEG]) for s in range(2)]
        decay = sb("s_decay", [P, 4, 4, SEG])
        ducopy = sb("s_ducopy", [P, 2, 4, CH])
        dl = sb("s_dl", [P, 2, 8, CH], BF16)
        duo_in = sb("s_du", [96, 2, 4, CH], BF16)
        Bs = sb("s_b", [P, 2, CH])
        Cs = sb("s_c", [P, 2, CH])
        window = [sb(f"s_window{s}", [P, CH * WIN]) for s in range(2)]
        a_w = sb("s_a", [P, PAIRS, P], BF16)
        sel = sb("s_sel", [96, 16, P], BF16)
        yout = sb("s_y", [P, 2, 2, 512])
        a_bank = ctx.enter_context(nc.psum_tensor("s_abank", [P, 2, 4, CH], F32))
        u_bank = ctx.enter_context(nc.psum_tensor("s_ubank", [P, 2, 2, CH], F32))
        y_bank = ctx.enter_context(nc.psum_tensor("s_ybank", [P, 2, 512], F32))

        loaded = [sem("loaded0"), sem("loaded1")]
        a_loaded = sem("a_w_loaded")
        sel_ready = sem("sel_ready")
        a_ready = sem("a_ready")
        exp_done = sem("decay_ready")
        u_ready = sem("spread_u_ready")
        u_copied = sem("u_copied")
        dbu_pool = sem("dbu_pool")
        dbu_dve = sem("dbu_dve")
        scan_done = sem("scan_done")
        carry_done = sem("carry_done")
        window_ready = sem("window_ready")
        y_ready = sem("y_ready")
        y_read = sem("y_read")
        yout_zero = sem("yout_zero")
        y_stored = [sem("y_stored0"), sem("y_stored1")]

        block = ctx.enter_context(nc.Block())

        set_quads = [FIRST_C + s * (QUADS - FIRST_C) // SETS for s in range(SETS)]

        def over_chunks(eng, chunk, at_group=None, at_batch=None):
            with eng.Fori(0, NG) as g:
                if at_group:
                    at_group(g)
                with eng.Fori(0, BATCH) as b:
                    if at_batch:
                        at_batch(g, b)
                    with eng.Fori(0, CPB // 2) as c:
                        for s in range(2):
                            chunk(g, b, (b * (CPB // 2) + c) * 2 + s, s)

        def number(g, i):
            return g * NB + i

        @block.sync
        def _(sp):
            def at_group(g):
                sp.wait_ge(u_ready, g * (NB * 2 * QUADS) + 4 * QUADS)
                sp.dma_start(a_w[:, :, :], d["a_image"][g]).then_inc(a_loaded, 16)

            def store(f, s):
                for ct in range(4):
                    dst = d["y"][f].rearrange("(e c r) k -> c r e k", e=SETS, c=4)[ct]
                    src = yout[32 * ct:32 * ct + WIN, s].rearrange("p o (e k) -> p (o e) k", k=64)
                    sp.dma_start(dst, src).then_inc(y_stored[s], 16)

            def chunk(g, b, i, s):
                f = number(g, i)
                sp.wait_ge(u_ready, f * (2 * QUADS) + 2 * QUADS)
                sp.wait_ge(dbu_pool, f * NA + NA)
                sp.wait_ge(dbu_dve, f * (2 * ND) + 2 * ND)
                t = bass.ds(i * CH, CH)
                for c, (_, j) in enumerate(COMBOS):
                    src = d["dparts"][j, bass.ds(g * P, P), t].rearrange("(r s) t -> r s t", s=8)
                    sp.dma_start(dl[16 * c:16 * c + 16, s], src).then_inc(loaded[s], 16)
                for j in range(3):
                    src = d["uparts"][j, bass.ds(g * P, P), t].rearrange("(r s) t -> r s t", s=4)
                    sp.dma_start(duo_in[32 * j:32 * j + 32, s], src).then_inc(loaded[s], 16)
                sp.dma_start(Bs[:, s], d["B"][:, t]).then_inc(loaded[s], 16)
                sp.dma_start(Cs[:, s], d["C"][:, t]).then_inc(loaded[s], 16)
                sp.wait_ge(y_read, f * 2 + 3)
                store(f, 1 - s)

            sp.wait_ge(yout_zero, 1)
            over_chunks(sp, chunk, at_group)
            last = NG * NB
            sp.wait_ge(y_read, last * 2 + 3)
            store(last, 1)
            sp.wait_ge(y_read, last * 2 + 5)
            store(last + 1, 0)
            sp.wait_ge(y_stored[0], 64 * (last // 2 + 2))
            sp.wait_ge(y_stored[1], 64 * (last // 2 + 1))

        @block.tensor
        def _(pe):
            pe.sem_inc(u_ready, 4 * QUADS)
            pe.wait_ge(sel_ready, 4)
            pe.wait_ge(y_read, 2)
            pe.sem_inc(y_ready, 2)

            def contract(f, e, s):
                half = e // (SETS // 2)
                if e == 0:
                    pe.wait_ge(scan_done, f * QUADS + QUADS)
                    pe.wait_ge(window_ready, f * 2 + 2)
                if e % (SETS // 2) == 0:
                    pe.wait_ge(y_read, f * 2 + 2 + half)
                col = (e % (SETS // 2)) * 64
                for tt in range(4):
                    for ct in range(4):
                        t = e * 16 + ct * 4 + tt
                        last = nc.tensor.matmul(y_bank[32 * ct:32 * ct + WIN, half, col:col + 64],
                                                window[s][:, t * WIN:(t + 1) * WIN], H[s][:, :, 1 + t],
                                                start=(tt == 0), stop=(tt == 3))
                if e % (SETS // 2) == SETS // 2 - 1:
                    last.then_inc(y_ready, 1)

            def chunk(g, b, i, s):
                f = number(g, i)
                pe.wait_ge(a_loaded, g * 16 + 16)
                pe.wait_ge(loaded[s], (f - s) * (8 * NL) + 16 * NL)
                for q in range(QUADS):
                    pe.wait_ge(exp_done, f * QUADS + q + 1)
                    for k in range(4):
                        last = nc.tensor.matmul(a_bank[:, q % 2, k, :], a_w[:, 4 * q + k, :],
                                                dl[:, s, (4 * q + k) % 8, :], start=True, stop=True)
                    last.then_inc(a_ready, 1)
                    for k in range(2):
                        r = (q - 1) % QUADS
                        if r in ACT_QUADS:
                            pe.wait_ge(u_copied, f * (2 * NA) + (2 * act_before[q] + k + 1))
                        else:
                            pe.wait_ge(dbu_dve, f * (2 * ND) + (4 * ND + 2 * dve_before[q] - 1 + k))
                        nc.tensor.matmul(u_bank[:, k], sel[:, q, :], duo_in[:, s, 2 * k:2 * k + 2, :],
                                         start=True, stop=True).then_inc(u_ready, 1)
                    for e in range(SETS):
                        if set_quads[e] == q:
                            contract(f, e, 1 - s)

            over_chunks(pe, chunk)
            for e in range(SETS):
                contract(NG * NB, e, 1)

        @block.scalar
        def _(act):
            act.sem_inc(exp_done, 2)
            act.sem_inc(u_copied, 2)
            act.sem_inc(y_stored[0], 64)

            def chunk(g, b, i, s):
                f = number(g, i)
                for q in range(QUADS):
                    act.wait_ge(a_ready, f * QUADS + q + 1)
                    act.wait_ge(scan_done, f * QUADS + q + QUADS - 3)
                    nc.scalar.activation(decay[:, q % 4, :, 1:SEG], a_bank[:, q % 2], ACT.Exp).then_inc(exp_done, 1)
                    if q in ACT_QUADS:
                        n = act_before[q]
                        act.wait_ge(dbu_pool, f * NA + n - 1 + 2 * NA)
                        for k in range(2):
                            act.wait_ge(u_ready, f * (2 * QUADS) + (4 * QUADS + 2 * q + k + 1))
                            nc.scalar.activation(ducopy[:, n % 2, 2 * k:2 * k + 2, :], u_bank[:, k],
                                                 ACT.Identity).then_inc(u_copied, 1)
                    if q == 1:
                        act.wait_ge(y_ready, f * 2 + 2)
                        nc.scalar.activation(yout[:, 1 - s, 1], y_bank[:, 1], ACT.Identity).then_inc(y_read, 1)
                    if q == 12:
                        act.wait_ge(y_stored[s], (f - s) * 32 + 64)
                        act.wait_ge(y_ready, f * 2 + 3)
                        nc.scalar.activation(yout[:, s, 0], y_bank[:, 0], ACT.Identity).then_inc(y_read, 1)

            act.wait_ge(yout_zero, 1)
            over_chunks(act, chunk)
            last = NG * NB
            act.wait_ge(y_ready, last * 2 + 2)
            nc.scalar.activation(yout[:, 1, 1], y_bank[:, 1], ACT.Identity).then_inc(y_read, 1)
            act.wait_ge(y_stored[0], last * 32 + 64)
            for half in range(2):
                act.wait_ge(y_ready, last * 2 + 3 + half)
                nc.scalar.activation(yout[:, 0, half], y_bank[:, half], ACT.Identity).then_inc(y_read, 1)

        @block.vector
        def _(dve):
            dve.sem_inc(dbu_dve, 4 * ND)
            for s in range(2):
                nc.vector.memset(y_bank[:, s], 0.0).then_inc(y_read, 1)
                nc.vector.memset(window[s][:, :], 0.0).then_inc(window_ready, 1)
            nc.vector.memset(decay[:, :, :, 0:1], 0.0).then_inc(carry_done, 1)
            nc.vector.memset(H[1][:, :, :], 0.0).then_inc(scan_done, QUADS)

            def at_batch(g, b):
                n = g * (NB + BATCH) + b * (CPB + 1)
                dve.wait_ge(carry_done, n + 1)
                nc.vector.memset(H[0][:, :, 0:1], 0.0).then_inc(carry_done, 1)

            def chunk(g, b, i, s):
                f = number(g, i)
                dve.wait_ge(loaded[s], (f - s) * (8 * NL) + 16 * NL)
                dve.wait_ge(y_ready, f * 2 + 2)
                dve.wait_ge(window_ready, f * 2 + 2)
                for p in range(2):
                    w = window[s][64 * p:64 * p + 64, :]
                    dst = bass.AP(w.tensor, w.offset + p, [list(w.ap[0]), [4 * WIN, CH // 4], [WIN + 2, 4]])
                    src = Cs[64 * p:64 * p + 64, s, :].rearrange("p (a c) -> p a c", c=4)
                    nc.vector.tensor_copy(dst, src).then_inc(window_ready, 1)
                for q in range(QUADS + LAG):
                    if q < QUADS and q not in ACT_QUADS:
                        for k in range(2):
                            r = 4 * q + 2 * k
                            dve.wait_ge(u_ready, f * (2 * QUADS) + (4 * QUADS + 2 * q + k + 1))
                            nc.vector.tensor_tensor(H[s][:, r:r + 2, 1:SEG], u_bank[:, k],
                                                    Bs[:, s:s + 1, :].broadcast_to([P, 2, CH]),
                                                    ALU.mult).then_inc(dbu_dve, 1)
                    r = q - LAG
                    if r < 0:
                        continue
                    if r == 0:
                        dve.wait_ge(carry_done, f + (g * BATCH + b) + 2)
                    dve.wait_ge(exp_done, f * QUADS + r + 3)
                    if r in ACT_QUADS:
                        dve.wait_ge(dbu_pool, f * NA + (2 * NA + act_before[r] + 1))
                    else:
                        dve.wait_ge(dbu_dve, f * (2 * ND) + (4 * ND + 2 * dve_before[r] + 2))
                    h = H[s][:, 4 * r:4 * r + 4, :].rearrange("p a t -> p (a t)")
                    nc.vector.tensor_tensor_scan(h, decay[:, r % 4].rearrange("p a t -> p (a t)"), h, 0.0,
                                                 ALU.mult, ALU.add).then_inc(scan_done, 1)
                dve.wait_ge(scan_done, f * QUADS + 2 * QUADS)
                nc.vector.tensor_copy(H[1 - s][:, :, 0:1], H[s][:, :, CH:SEG]).then_inc(carry_done, 1)

            over_chunks(dve, chunk, at_batch=at_batch)

        @block.gpsimd
        def _(pool):
            pool.sem_inc(dbu_pool, 2 * NA)
            nc.gpsimd.memset(yout[:, 1], 0.0).then_inc(yout_zero, 1)
            nc.gpsimd.memset(sel[:, :, :], 0.0).then_inc(sel_ready, 1)
            pool.wait_ge(sel_ready, 1)
            v = sel[:, :, :].rearrange("p q (h n) -> p q h n", h=2)
            for j in range(3):
                pool.wait_ge(sel_ready, j + 1)
                nc.gpsimd.affine_select(out=v, in_=v, compare_op=ALU.not_equal, fill=1.0, base=-32 * j,
                                        pattern=[[-1, 16], [-16, 2], [0, NS]],
                                        channel_multiplier=1).then_inc(sel_ready, 1)

            def chunk(g, b, i, s):
                f = number(g, i)
                pool.wait_ge(loaded[s], (f - s) * (8 * NL) + 16 * NL)
                pool.wait_ge(y_ready, f * 2 + 2)
                for n, q in enumerate(ACT_QUADS):
                    pool.wait_ge(u_copied, f * (2 * NA) + 2 * n + 4)
                    nc.gpsimd.tensor_tensor(H[s][:, 4 * q:4 * q + 4, 1:SEG], ducopy[:, n % 2],
                                            Bs[:, s:s + 1, :].broadcast_to([P, 4, CH]),
                                            ALU.mult).then_inc(dbu_pool, 1)

            over_chunks(pool, chunk)


def output_stage(nc, d):
    with ExitStack() as ctx:
        def sb(name, shape, dt=F32):
            return ctx.enter_context(nc.sbuf_tensor(name, shape, dt))

        def sem(name):
            return ctx.enter_context(nc.semaphore(name))

        raw = sb("o_raw", [P, 3, MH * DM], I32)
        wf = sb("o_wf", [P, 3, MH * DM])
        wg = sb("o_wg", [P, KD, HID])
        wu = sb("o_wu", [P, KD, HID])
        wd = sb("o_wd", [P, MH, DM])
        w_out = sb("o_w_out", [P, MI, DM])
        dskip = sb("o_dskip", [P, MI])
        half = sb("o_half", [P, SUB])
        spare = sb("o_spare", [P, 1])
        ident = sb("o_ident", [P, P])
        y = sb("o_y", [P, SUB, NG, P])
        u = sb("o_u", [P, MI, TW])
        sz = sb("o_sz", [P, MI, TW])
        yg = sb("o_yg", [P, MI, TW])
        res = sb("o_res", [P, SUB, DM])
        x1 = sb("o_x1", [P, 2, SUB, DM])
        xf = sb("o_xf", [P, SUB, DM])
        xfT = sb("o_xfT", [P, KD, TW])
        stats = sb("o_stats", [P, SUB, 6])
        mv = sb("o_mv", [P, SUB, 2])
        veps = sb("o_veps", [P, SUB])
        rstd = sb("o_rstd", [P, SUB])
        sg = sb("o_sg", [P, 2, TW])
        hid = sb("o_hid", [P, MH, TW])
        out = sb("o_out", [P, SUB, DM])
        tr = ctx.enter_context(nc.psum_tensor("o_tr", [P, 2, TW], F32))
        gu = ctx.enter_context(nc.psum_tensor("o_gu", [P, 2, 2, TW], F32))
        ob = ctx.enter_context(nc.psum_tensor("o_ob", [P, SUB, DM], F32))

        w_loaded = sem("w_loaded")
        consts = sem("o_consts")
        w_scaled = sem("w_scaled")
        w_turned = sem("w_turned")
        w_read = sem("w_read")
        y_loaded, u_loaded, sz_loaded = sem("y_loaded"), sem("u_loaded"), sem("sz_loaded")
        res_loaded = sem("res_loaded")
        tr_ready = sem("o_tr_ready")
        y_taken = sem("y_taken")
        xf_taken = sem("xf_taken")
        gated = sem("gated")
        proj_ready = sem("proj_ready")
        x1_done = sem("x1_done")
        stats_done, mv_done, veps_done = sem("o_stats_done"), sem("o_mv_done"), sem("o_veps_done")
        rstd_done = sem("o_rstd_done")
        xf_done = sem("xf_done")
        gu_ready = sem("gu_ready")
        silu_done = sem("silu_done")
        hid_done = sem("hid_done")
        down_ready = sem("down_ready")
        out_done = sem("out_done")
        out_stored = sem("out_stored")

        block = ctx.enter_context(nc.Block())
        n_turns = 3 * KD * MH

        def over_tiles(eng, first, second):
            for k in range(3):
                first(0, 0, k)

            def step(i, s):
                for k in range(3):
                    first(i + 1, 1 - s, k)
                    second(i, s, k)

            with eng.Fori(0, NT // 2 - 1) as j:
                for s in range(2):
                    step(j * 2 + s, s)
            step(NT - 2, 0)
            for k in range(3):
                second(NT - 1, 1, k, True)

        def nothing(i, s, k, last_tile=False):
            pass

        def turned(n):
            w, r = n // (KD * MH), n % (KD * MH)
            if w < 2:
                m, k = r // KD, r % KD
                return wf[:, w, m * DM + k * P:m * DM + (k + 1) * P], (wg, wu)[w][:, k, m * P:(m + 1) * P]
            k, m = r // MH, r % MH
            return wf[:, 2, k * HID + m * P:k * HID + (m + 1) * P], wd[:, m, k * P:(k + 1) * P]

        @block.sync
        def _(sp):
            for w, name in enumerate(("w_gate", "w_up")):
                sp.dma_start(raw[:, w].rearrange("p (m c) -> p m c", c=DM),
                             d[name].rearrange("(m p) c -> p m c", p=P)).then_inc(w_loaded, 16)
            sp.dma_start(raw[:, 2].rearrange("p (k h) -> p k h", h=HID),
                         d["w_down"].rearrange("(k p) h -> p k h", p=P)).then_inc(w_loaded, 16)
            sp.dma_start(w_out[:, :, :], d["W_out"].rearrange("(m p) n -> p m n", p=P)).then_inc(w_loaded, 16)
            sp.dma_start(dskip[:, :], d["D"].rearrange("(m p) -> p m", p=P), allow_slow_non_contiguous=True).then_inc(w_loaded, 16)

            yv = d["y"].rearrange("f (t h) k -> f t (h k)", h=2)

            def tile_of(dram, i):
                return dram.rearrange("(m p) t -> p m t", p=P)[:, :, bass.ds(i * TW, TW)]

            def first(i, s, k):
                if k != 0:
                    return
                sp.wait_ge(tr_ready, i * 6 + 2)
                for m in range(NG):
                    src = yv[bass.ds(i * 2 + (2 + m * NB), 2)].rearrange("f (s p) c -> p (f s) c", p=P)
                    sp.dma_start(y[:, :, m, :], src).then_inc(y_loaded, 16)
                sp.wait_ge(gated, i * 4 + 4)
                sp.dma_start(u[:, :, :], tile_of(d["u"], i)).then_inc(u_loaded, 16)
                sp.dma_start(sz[:, :, :], tile_of(d["sz"], i)).then_inc(sz_loaded, 16)
                sp.wait_ge(x1_done, i + 1)
                sp.dma_start(res[:, :, :], d["res"].rearrange("(i s p) c -> i p s c", s=SUB, p=P)[i]
                             ).then_inc(res_loaded, 16)

            def second(i, s, k, last_tile=False):
                if k != 2:
                    return
                sp.wait_ge(out_done, i + 3)
                sp.dma_start(d["out"].rearrange("(i s p) c -> i p s c", s=SUB, p=P)[i],
                             out[:, :, :]).then_inc(out_stored, 16)

            over_tiles(sp, first, second)
            sp.wait_ge(out_stored, 16 * (NT + 1))

        @block.tensor
        def _(pe):
            pe.wait_ge(consts, 3)
            pe.wait_ge(w_scaled, 3)
            for n in range(n_turns):
                if n >= 2:
                    pe.wait_ge(w_read, n - 1)
                nc.tensor.transpose(tr[:, n % 2, 0:P], turned(n)[0], ident[:, :]).then_inc(w_turned, 1)
            pe.wait_ge(w_read, n_turns)
            pe.sem_inc(tr_ready, 4)
            pe.sem_inc(gu_ready, MH)
            pe.sem_inc(proj_ready, 1)
            pe.sem_inc(down_ready, 1)
            pe.wait_ge(w_loaded, 80)

            def first(i, s, k):
                if k == 0:
                    pe.wait_ge(y_loaded, i * 64 + 64)
                    for m in range(MI):
                        if m < 2:
                            pe.wait_ge(xf_taken, i * 2 + m + 1)
                        else:
                            pe.wait_ge(y_taken, i * 4 + m + 3)
                        for g in range(SUB):
                            last = nc.tensor.transpose(tr[:, m % 2, g * P:(g + 1) * P], y[:, g, m, :], ident[:, :])
                        last.then_inc(tr_ready, 1)
                if k == 1:
                    pe.wait_ge(gated, i * 4 + 8)
                    pe.wait_ge(out_done, i + 1)
                    pe.wait_ge(x1_done, i + 1)
                    for g in range(SUB):
                        for m in range(MI):
                            last = nc.tensor.matmul(ob[:, g, :], yg[:, m, g * P:(g + 1) * P], w_out[:, m, :],
                                                    start=(m == 0), stop=(m == MI - 1))
                    last.then_inc(proj_ready, 1)
                if k == 2:
                    pe.wait_ge(xf_done, i * 4 + 4)
                    pe.wait_ge(y_taken, i * 4 + 8)
                    for kk in range(KD):
                        for g in range(SUB):
                            last = nc.tensor.transpose(tr[:, kk, g * P:(g + 1) * P],
                                                       xf[:, g, kk * P:(kk + 1) * P], ident[:, :])
                        last.then_inc(tr_ready, 1)

            def second(i, s, k, last_tile=False):
                if k < 2:
                    if k == 0:
                        pe.wait_ge(xf_taken, i * 2 + 4)
                    for m in range(3 * k, 3 * k + 3):
                        pe.wait_ge(hid_done, i * 6 + m + 5)
                        for r, w in enumerate((wg, wu)):
                            for kk in range(KD):
                                last = nc.tensor.matmul(gu[:, m % 2, r, :], w[:, kk, m * P:(m + 1) * P],
                                                        xfT[:, kk, :], start=(kk == 0), stop=(kk == KD - 1))
                        last.then_inc(gu_ready, 1)
                else:
                    pe.wait_ge(hid_done, i * 6 + 12)
                    pe.wait_ge(x1_done, NT + 1 if last_tile else i + 3)
                    for g in range(SUB):
                        for m in range(MH):
                            last = nc.tensor.matmul(ob[:, g, :], hid[:, m, g * P:(g + 1) * P], wd[:, m, :],
                                                    start=(m == 0), stop=(m == MH - 1))
                    last.then_inc(down_ready, 1)

            over_tiles(pe, first, second)

        @block.scalar
        def _(act):
            for n in range(n_turns):
                act.wait_ge(w_turned, n + 1)
                nc.scalar.activation(turned(n)[1], tr[:, n % 2, 0:P], ACT.Identity).then_inc(w_read, 1)
            act.sem_inc(xf_taken, 2)
            act.sem_inc(out_stored, 16)

            def first(i, s, k):
                if k != 2:
                    return
                act.wait_ge(gu_ready, i * MH + MH)
                for kk in range(KD):
                    act.wait_ge(tr_ready, i * 6 + 9 + kk)
                    nc.scalar.activation(xfT[:, kk, :], tr[:, kk, :], ACT.Identity).then_inc(xf_taken, 1)

            def second(i, s, k, last_tile=False):
                if k == 2:
                    return
                for m in range(3 * k, 3 * k + 3):
                    act.wait_ge(gu_ready, i * MH + MH + m + 1)
                    act.wait_ge(hid_done, i * MH + m + 5)
                    nc.scalar.activation(sg[:, m % 2, :], gu[:, m % 2, 0, :], ACT.Silu).then_inc(silu_done, 1)

            over_tiles(act, first, second)

        @block.vector
        def _(dve):
            for w in range(3):
                dve.wait_ge(w_loaded, 80)
                nc.vector.tensor_scalar(wf[:, w], raw[:, w], WSCALE, None, ALU.mult).then_inc(w_scaled, 1)
            dve.sem_inc(y_taken, 4)
            dve.sem_inc(gated, 4)
            dve.sem_inc(x1_done, 1)
            dve.sem_inc(hid_done, MH)
            dve.sem_inc(out_done, 2)

            def first(i, s, k):
                if k == 0:
                    dve.wait_ge(u_loaded, i * 16 + 16)
                    dve.wait_ge(sz_loaded, i * 16 + 16)
                    dve.wait_ge(proj_ready, i + 1)
                    for m in range(MI):
                        dve.wait_ge(tr_ready, i * 6 + 5 + m)
                        nc.vector.scalar_tensor_tensor(out=yg[:, m, :], in0=u[:, m, :], scalar=dskip[:, m:m + 1],
                                                       in1=tr[:, m % 2, :], op0=ALU.mult,
                                                       op1=ALU.add).then_inc(y_taken, 1)
                    for m in range(MI):
                        dve.wait_ge(y_taken, i * 4 + 5 + m)
                        nc.vector.tensor_tensor(yg[:, m, :], yg[:, m, :], sz[:, m, :], ALU.mult).then_inc(gated, 1)
                if k == 1:
                    dve.wait_ge(res_loaded, i * 16 + 16)
                    dve.wait_ge(proj_ready, i + 2)
                    nc.vector.tensor_tensor(x1[:, s], ob[:, :, :], res[:, :, :], ALU.add).then_inc(x1_done, 1)
                    dve.wait_ge(x1_done, i + 2)
                    for g in range(SUB):
                        nc.vector.bn_stats(stats[:, g, :], x1[:, s, g, :]).then_inc(stats_done, 1)
                    dve.wait_ge(stats_done, i * 4 + 4)
                    nc.vector.memset(spare[:, 0:1], 0.0)
                    for g in range(SUB):
                        nc.vector.bn_aggr(mv[:, g, :], stats[:, g, :]).then_inc(mv_done, 1)
                    dve.wait_ge(mv_done, i * 4 + 4)
                    nc.vector.tensor_scalar(veps[:, :], mv[:, :, 1], EPS, None, ALU.add).then_inc(veps_done, 1)
                    dve.wait_ge(rstd_done, i + 1)
                    dve.wait_ge(tr_ready, i * 6 + 4)
                    for g in range(SUB):
                        nc.vector.tensor_scalar(xf[:, g, :], x1[:, s, g, :], mv[:, g, 0:1], rstd[:, g:g + 1],
                                                ALU.subtract, ALU.mult).then_inc(xf_done, 1)

            def second(i, s, k, last_tile=False):
                if k < 2:
                    if k == 0:
                        dve.wait_ge(down_ready, i + 1)
                    for m in range(3 * k, 3 * k + 3):
                        dve.wait_ge(silu_done, i * MH + m + 1)
                        nc.vector.tensor_tensor(hid[:, m, :], sg[:, m % 2, :], gu[:, m % 2, 1, :],
                                                ALU.mult).then_inc(hid_done, 1)
                else:
                    dve.wait_ge(down_ready, i + 2)
                    dve.wait_ge(out_stored, i * 16 + 16)
                    nc.vector.tensor_tensor(out[:, :, :], ob[:, :, :], x1[:, s], ALU.add).then_inc(out_done, 1)

            over_tiles(dve, first, second)

        @block.gpsimd
        def _(pool):
            nc.gpsimd.memset(half[:, :], -0.5).then_inc(consts, 1)
            nc.gpsimd.memset(ident[:, :], 0.0).then_inc(consts, 1)
            pool.wait_ge(consts, 2)
            nc.gpsimd.affine_select(out=ident[:, :], in_=ident[:, :], compare_op=ALU.not_equal, fill=1.0, base=0,
                                    pattern=[[-1, P]], channel_multiplier=1).then_inc(consts, 1)
            with pool.Fori(0, NT) as i:
                pool.wait_ge(veps_done, i + 1)
                nc.gpsimd.tensor_tensor(rstd[:, :], veps[:, :], half[:, :], ALU.pow).then_inc(rstd_done, 1)


def build(nc, d):
    d = dict(d)

    def scratch(name, shape, dt=F32):
        d[name] = nc.dram_tensor(f"scratch_{name}", shape, dt, kind="Internal").ap()

    scratch("res", [TOK, DM])
    scratch("u", [DI, TOK])
    scratch("sz", [DI, TOK])
    scratch("B", [P, TOK])
    scratch("C", [P, TOK])
    scratch("dparts", [3, DI, TOK], BF16)
    scratch("uparts", [3, DI, TOK], BF16)
    scratch("a_parts", [3, DI, NS], BF16)
    scratch("a_image", [NG, P, PAIRS * P], BF16)
    scratch("y", [2 + NG * NB, 2 * CH, 64])
    with nc.sbuf_tensor("xnT", [P, KD, TOK], F32) as xnT:
        decay_stage(nc, d)
        norm_stage(nc, d, xnT)
        project_stage(nc, d, xnT)
    scan_stage(nc, d)
    output_stage(nc, d)


_INS = ["x", "ln_w", "ln_b", "W_in", "conv_w", "conv_b", "W_xproj", "W_dt", "b_dt", "A_log", "D", "W_out"]
_FFN = ["w_gate", "w_up", "w_down"]


def kernel(**inputs):
    import numpy as np
    import concourse.bacc as bacc
    from concourse.bass_utils import run_bass_kernel_spmd

    nc = bacc.Bacc("TRN2", target_bir_lowering=False, num_devices=1, dynamic_dma_scratch_size=1024)
    arrays, d = {}, {}
    for name, key in [(n, f"L0_attn_{n}") for n in _INS] + [(n, f"L0_ffn_{n}") for n in _FFN]:
        a = np.ascontiguousarray(inputs[key])
        arrays[f"in_{name}"] = a
        d[name] = nc.dram_tensor(f"in_{name}", a.shape, mybir.dt.from_np(a.dtype), kind="ExternalInput").ap()
    d["x"] = d["x"].rearrange("b t c -> (b t) c")
    out = nc.dram_tensor("out", (BATCH, SEQ, DM), F32, kind="ExternalOutput").ap()
    d["out"] = out.rearrange("b t c -> (b t) c")
    build(nc, d)
    return run_bass_kernel_spmd(nc, [arrays], core_ids=[0]).results[0]["out"]
```

```python
from contextlib import ExitStack

import concourse.bass as bass
from concourse import mybir

ALU = mybir.AluOpType
ACT = mybir.ActivationFunctionType
F32 = mybir.dt.float32
BF16 = mybir.dt.bfloat16
I32 = mybir.dt.int32

P = 128
BATCH, SEQ, DM = 4, 2048, 256
DI, NS, RANK, TAPS = 512, 64, 16, 4
HID = 768
TOK = BATCH * SEQ
EPS = 1e-5
WSCALE = 1.0 / 127.0

TW = 512
NT = TOK // TW
TPB = SEQ // TW
SUB = TW // P
KD = DM // P
MI = DI // P
MH = HID // P

CH = 256
NB = TOK // CH
CPB = SEQ // CH
NG = DI // P
PAIRS = P // 2
QUADS = PAIRS // 4
SEG = CH + 1
COMBOS = [(i, j) for j in range(3) for i in range(3) if i + j < 4]
WSTEPS = 8
WIN = 2 * WSTEPS
SETS = CH // 16
DIRECT = [4, 6, 7, 10, 11, 14, 17, 20, 22, 26, 29, 31]
COPIED = [n for n in range(2 * QUADS) if n not in DIRECT]
U_BANKS = 3
COPIES = 4
RING = 4
LAG = 2
FIRST_C = 3
WINDOW_QUAD = 2
UNROLL = 4
Y_QUAD = 1


def norm_stage(nc, d, xnT):
    with ExitStack() as ctx:
        def sb(name, shape, dt=F32):
            return ctx.enter_context(nc.sbuf_tensor(name, shape, dt))

        def sem(name):
            return ctx.enter_context(nc.semaphore(name))

        x = sb("n_x", [P, 2, SUB, DM])
        xa = sb("n_xa", [P, 2, SUB, DM])
        xn = sb("n_xn", [P, 2, SUB, DM])
        res = sb("n_res", [P, 2, SUB, DM])
        stats = sb("n_stats", [P, 2, 2, SUB, 6])
        mv = sb("n_mv", [P, 2, 2, SUB, 2])
        veps = sb("n_veps", [P, 2, 2, SUB])
        rstd = sb("n_rstd", [P, 2, 2, SUB])
        half = sb("n_half", [P, SUB])
        spare = sb("n_spare", [P, 1])
        ident = sb("n_ident", [P, P])
        lnw = sb("n_lnw", [P, KD])
        lnb = sb("n_lnb", [P, KD])
        tr = ctx.enter_context(nc.psum_tensor("n_tr", [P, 2, KD, TW], F32))

        x_loaded = [sem("x_loaded0"), sem("x_loaded1")]
        par_loaded = sem("par_loaded")
        consts = sem("consts")
        stats_done = sem("stats_done")
        mv_done = sem("mv_done")
        veps_done = sem("veps_done")
        rstd_done = sem("rstd_done")
        xa_done = sem("xa_done")
        xn_done = sem("xn_done")
        res_done = sem("res_done")
        res_stored = [sem("res_stored0"), sem("res_stored1")]
        tr_done = sem("tr_done")
        tr_read = sem("tr_read")

        block = ctx.enter_context(nc.Block())
        xv = d["x"].rearrange("(i s p) c -> i p s c", s=SUB, p=P)
        rv = d["res"].rearrange("(i s p) c -> i p s c", s=SUB, p=P)

        @block.sync
        def _(sp):
            sp.dma_start(lnw[:, :], d["ln_w"].rearrange("(k p) -> p k", p=P), allow_slow_non_contiguous=True).then_inc(par_loaded, 16)
            sp.dma_start(lnb[:, :], d["ln_b"].rearrange("(k p) -> p k", p=P), allow_slow_non_contiguous=True).then_inc(par_loaded, 16)
            with sp.Fori(0, NT // 2) as j:
                for s in range(2):
                    sp.wait_ge(res_done, j * 2 + s + 1)
                    sp.dma_start(x[:, s], xv[j * 2 + s]).then_inc(x_loaded[s], 16)

        @block.vector
        def _(dve):
            def layernorm(j, s, k, src, dst, done):
                i = j * 2 + s
                for g in range(SUB):
                    nc.vector.bn_stats(stats[:, s, k, g, :], src[:, s, g, :]).then_inc(stats_done, 1)
                n = j * 16 + k * 8 + s * 4
                dve.wait_ge(stats_done, n + 4)
                nc.vector.memset(spare[:, 0:1], 0.0)
                for g in range(SUB):
                    nc.vector.bn_aggr(mv[:, s, k, g, :], stats[:, s, k, g, :]).then_inc(mv_done, 1)
                dve.wait_ge(mv_done, n + 4)
                nc.vector.tensor_scalar(veps[:, s, k, :], mv[:, s, k, :, 1], EPS, None, ALU.add).then_inc(veps_done, 1)

            def scaled(j, s, k, src, dst, done):
                dve.wait_ge(rstd_done, j * 4 + k * 2 + s + 1)
                for g in range(SUB):
                    nc.vector.tensor_scalar(dst[:, s, g, :], src[:, s, g, :], mv[:, s, k, g, 0:1],
                                            rstd[:, s, k, g:g + 1], ALU.subtract, ALU.mult).then_inc(done, 1)

            with dve.Fori(0, NT // 2) as j:
                for s in range(2):
                    dve.wait_ge(x_loaded[s], j * 16 + 16)
                    layernorm(j, s, 0, x, xa, xa_done)
                for s in range(2):
                    dve.wait_ge(res_done, j * 2 + s + 1)
                    scaled(j, s, 0, x, xa, xa_done)
                for s in range(2):
                    dve.wait_ge(xa_done, j * 8 + s * 4 + 4)
                    layernorm(j, s, 1, xa, xn, xn_done)
                for s in range(2):
                    dve.wait_ge(tr_done, j * 2 + s + 1)
                    scaled(j, s, 1, xa, xn, xn_done)

        @block.gpsimd
        def _(pool):
            nc.gpsimd.memset(half[:, :], -0.5).then_inc(consts, 1)
            nc.gpsimd.memset(ident[:, :], 0.0).then_inc(consts, 1)
            pool.wait_ge(consts, 2)
            nc.gpsimd.affine_select(out=ident[:, :], in_=ident[:, :], compare_op=ALU.not_equal, fill=1.0, base=0,
                                    pattern=[[-1, P]], channel_multiplier=1).then_inc(consts, 1)
            pool.sem_inc(res_done, 2)
            with pool.Fori(0, NT // 2) as j:
                for k in range(2):
                    for s in range(2):
                        pool.wait_ge(veps_done, j * 4 + k * 2 + s + 1)
                        nc.gpsimd.tensor_tensor(rstd[:, s, k, :], veps[:, s, k, :], half[:, :],
                                                ALU.pow).then_inc(rstd_done, 1)
                for s in range(2):
                    pool.wait_ge(xn_done, j * 8 + s * 4 + 4)
                    pool.wait_ge(res_stored[s], j * 16 + 16)
                    nc.gpsimd.tensor_tensor(res[:, s], x[:, s], xa[:, s], ALU.add).then_inc(res_done, 1)

        @block.tensor
        def _(pe):
            pe.wait_ge(consts, 3)
            pe.sem_inc(tr_done, 2)
            with pe.Fori(0, NT // 2) as j:
                for s in range(2):
                    pe.wait_ge(xn_done, j * 8 + s * 4 + 4)
                    pe.wait_ge(tr_read, j * 4 + s * 2 + 2)
                    for k in range(KD):
                        for g in range(SUB):
                            last = nc.tensor.transpose(tr[:, s, k, g * P:(g + 1) * P],
                                                       xn[:, s, g, k * P:(k + 1) * P], ident[:, :])
                    last.then_inc(tr_done, 1)

        @block.scalar
        def _(act):
            act.sem_inc(tr_read, 4)
            act.sem_inc(res_stored[0], 16)
            act.sem_inc(res_stored[1], 16)
            act.wait_ge(par_loaded, 32)
            with act.Fori(0, NT // 2) as j:
                for s in range(2):
                    act.wait_ge(tr_done, j * 2 + s + 3)
                    for k in range(KD):
                        nc.scalar.activation(xnT[:, k, bass.ds((j * 2 + s) * TW, TW)], tr[:, s, k, :], ACT.Identity,
                                             bias=lnb[:, k:k + 1], scale=lnw[:, k:k + 1]).then_inc(tr_read, 1)
                    act.wait_ge(res_done, j * 2 + s + 3)
                    act.dma_start(rv[j * 2 + s], res[:, s]).then_inc(res_stored[s], 16)
            for s in range(2):
                act.wait_ge(res_stored[s], 16 * (NT // 2 + 1))


def decay_stage(nc, d):
    with ExitStack() as ctx:
        def sb(name, shape, dt=F32):
            return ctx.enter_context(nc.sbuf_tensor(name, shape, dt))

        def sem(name):
            return ctx.enter_context(nc.semaphore(name))

        a = sb("d_a", [P, MI, NS])
        parts = sb("d_parts", [P, 3, MI, NS], BF16)
        zeros = sb("d_zeros", [P, PAIRS * P // 2])
        a_loaded = sem("a_loaded")
        a_exp = sem("a_exp")
        a_step = sem("a_step")
        zeroed = sem("zeroed")
        image_zero = sem("image_zero")
        parts_stored = sem("parts_stored")
        placed = sem("placed")
        block = ctx.enter_context(nc.Block())

        @block.gpsimd
        def _(pool):
            nc.gpsimd.memset(zeros[:, :], 0.0).then_inc(zeroed, 1)

        @block.scalar
        def _(act):
            act.wait_ge(a_loaded, 16)
            nc.scalar.activation(a[:, :, :], a[:, :, :], ACT.Exp).then_inc(a_exp, 1)

        @block.vector
        def _(dve):
            count = [0]

            def step(ins):
                count[0] += 1
                ins.then_inc(a_step, 1)
                dve.wait_ge(a_step, count[0])

            dve.wait_ge(a_exp, 1)
            step(nc.vector.tensor_scalar(a[:, :, :], a[:, :, :], -1.0, -3.0e38, ALU.mult, ALU.max))
            step(nc.vector.tensor_copy(parts[:, 0], a[:, :, :]))
            step(nc.vector.tensor_tensor(a[:, :, :], a[:, :, :], parts[:, 0], ALU.subtract))
            step(nc.vector.tensor_copy(parts[:, 1], a[:, :, :]))
            step(nc.vector.tensor_tensor(parts[:, 2], a[:, :, :], parts[:, 1], ALU.subtract))

        @block.sync
        def _(sp):
            sp.dma_start(a[:, :, :], d["A_log"].rearrange("(m p) n -> p m n", p=P)).then_inc(a_loaded, 16)
            sp.wait_ge(zeroed, 1)
            for g in range(NG):
                sp.dma_start(d["a_image"][g], zeros[:, :].bitcast(BF16)).then_inc(image_zero, 16)
            sp.wait_ge(a_step, 5)
            for k in range(3):
                sp.dma_start(d["a_parts"][k].rearrange("(m p) n -> p m n", p=P),
                             parts[:, k]).then_inc(parts_stored, 16)
            sp.wait_ge(parts_stored, 48)
            sp.wait_ge(image_zero, 16 * NG)
            row = PAIRS * P
            image = d["a_image"].tensor
            for g in range(NG):
                for c, (i, _) in enumerate(COMBOS):
                    for h in range(2):
                        dst = bass.AP(image, (g * P + c * 16 + 8 * h) * row + NS * h,
                                      [[row + 8 * P, 8], [P, 8], [1, NS]])
                        src = d["a_parts"][i, g * P + 64 * h:g * P + 64 * h + 64, :].rearrange("(k s) n -> k s n", k=8)
                        sp.dma_start(dst, src).then_inc(placed, 16)
            sp.wait_ge(placed, 16 * NG * len(COMBOS) * 2)


def project_stage(nc, d, xnT):
    with ExitStack() as ctx:
        def sb(name, shape, dt=F32):
            return ctx.enter_context(nc.sbuf_tensor(name, shape, dt))

        def sem(name):
            return ctx.enter_context(nc.semaphore(name))

        w_in = sb("p_w_in", [P, KD, 2 * DI])
        w_x = sb("p_w_x", [P, MI, RANK + 4 * NS])
        w_dt = sb("p_w_dt", [RANK, DI])
        conv_w = sb("p_conv_w", [P, MI, TAPS])
        conv_b = sb("p_conv_b", [P, MI])
        b_dt = sb("p_b_dt", [P, MI])
        xi = sb("p_xi", [P, MI, TAPS - 1 + TW])
        acc = sb("p_acc", [P, MI, TW])
        u = sb("p_u", [P, 2, MI, TW])
        sz = sb("p_sz", [P, 2, MI, TW])
        dtr = sb("p_dtr", [RANK, TW])
        bc = sb("p_bc", [P, 2, 2, TW])
        v = sb("p_v", [P, MI, TW])
        ex = sb("p_ex", [P, MI, TW])
        w1 = sb("p_w1", [P, MI, TW])
        lw = sb("p_lw", [P, MI, TW])
        du = sb("p_du", [P, MI, TW])
        du_rest = sb("p_du_rest", [P, MI, TW])
        dparts = sb("p_dparts", [P, 3, MI, TW], BF16)
        uparts = sb("p_uparts", [P, 3, MI, TW], BF16)
        in_bank = ctx.enter_context(nc.psum_tensor("p_in", [P, 4, TW], F32))
        bk_bank = ctx.enter_context(nc.psum_tensor("p_bk", [P, 4, TW], F32))

        weights = sem("weights")
        in_ready = sem("in_ready")
        in_read = sem("in_read")
        xi_free = sem("xi_free")
        conv_step = sem("conv_step")
        conv_done = sem("conv_done")
        u_ready = sem("u_ready")
        back_ready = sem("back_ready")
        back_read = sem("back_read")
        abs_done = sem("abs_done")
        exp_done = sem("exp_done")
        w1_done = sem("w1_done")
        ln_done = sem("ln_done")
        tail_done = sem("tail_done")
        log_done = sem("log_done")
        delta_done = sem("delta_done")
        du_done = sem("du_done")
        d1_done, dr_done, d2_done = sem("d1_done"), sem("dr_done"), sem("d2_done")
        d3_done = sem("d3_done")
        u1_done, ur_done, u2_done = sem("u1_done"), sem("ur_done"), sem("u2_done")
        u3_done = sem("u3_done")
        u_stored = [sem("u_stored0"), sem("u_stored1")]
        sz_stored = [sem("sz_stored0"), sem("sz_stored1")]
        bc_stored = [sem("bc_stored0"), sem("bc_stored1")]
        dparts_stored = sem("dparts_stored")
        uparts_stored = sem("uparts_stored")
        n_weights = 10

        block = ctx.enter_context(nc.Block())

        def over_tiles(eng, step):
            def batch(b, last):
                for c in range(TPB):
                    def at(c):
                        if c < TPB:
                            return b * TPB + c, c, b
                        return None if last else ((b + 1) * TPB + (c - TPB), c - TPB, b + 1)
                    step(b * TPB + c, c, b, at(c + 1), at(c + 2))

            with eng.Fori(0, BATCH - 1) as b:
                batch(b, False)
            batch(BATCH - 1, True)

        @block.sync
        def _(sp):
            wx = d["W_xproj"].rearrange("(m p) n -> p m n", p=P)
            sp.dma_start(w_in[:, :, :], d["W_in"].rearrange("(k p) n -> p k n", p=P)).then_inc(weights, 16)
            sp.dma_start(w_x[:, :, 0:RANK], wx[:, :, 0:RANK]).then_inc(weights, 16)
            for r in range(4):
                at, frm = RANK + NS * r, RANK + NS * (r // 2)
                sp.dma_start(w_x[:, :, at:at + NS], wx[:, :, frm:frm + NS]).then_inc(weights, 16)
            sp.dma_start(w_dt[:, :], d["W_dt"]).then_inc(weights, 16)
            sp.dma_start(conv_w[:, :, :], d["conv_w"].rearrange("(m p) o k -> p m (o k)", p=P)).then_inc(weights, 16)
            sp.dma_start(conv_b[:, :], d["conv_b"].rearrange("(m p) -> p m", p=P), allow_slow_non_contiguous=True).then_inc(weights, 16)
            sp.dma_start(b_dt[:, :], d["b_dt"].rearrange("(m p) -> p m", p=P), allow_slow_non_contiguous=True).then_inc(weights, 16)

            def tile_of(dram, i):
                return dram.rearrange("(m p) t -> p m t", p=P)[:, :, bass.ds(i * TW, TW)]

            def front_stores(i, c, b):
                sp.wait_ge(in_read, i * 8 + 12)
                sp.dma_start(tile_of(d["sz"], i), sz[:, c % 2]).then_inc(sz_stored[c % 2], 16)
                sp.wait_ge(u_ready, i * 4 + 8)
                sp.dma_start(tile_of(d["u"], i), u[:, c % 2]).then_inc(u_stored[c % 2], 16)

            def back_stores(i, c, b):
                sp.wait_ge(back_read, i * 7 + 10)
                sp.dma_start(d["B"][:, bass.ds(i * TW, TW)], bc[:, c % 2, 0, :]).then_inc(bc_stored[c % 2], 16)
                sp.wait_ge(d3_done, i + 2)
                sp.dma_start(d["C"][:, bass.ds(i * TW, TW)], bc[:, c % 2, 1, :]).then_inc(bc_stored[c % 2], 16)
                for k in range(3):
                    sp.dma_start(tile_of(d["dparts"][k], i), dparts[:, k]).then_inc(dparts_stored, 16)
                sp.wait_ge(u3_done, i + 2)
                for k in range(3):
                    sp.dma_start(tile_of(d["uparts"][k], i), uparts[:, k]).then_inc(uparts_stored, 16)

            def step(i, c, b, ahead1, ahead2):
                if ahead1:
                    front_stores(*ahead1)
                back_stores(i, c, b)

            front_stores(0, 0, 0)
            over_tiles(sp, step)
            for s in range(2):
                sp.wait_ge(u_stored[s], 16 * (NT // 2 + 1))
                sp.wait_ge(sz_stored[s], 16 * (NT // 2 + 1))
                sp.wait_ge(bc_stored[s], 32 * (NT // 2 + 1))
            sp.wait_ge(dparts_stored, 48 * (NT + 1))
            sp.wait_ge(uparts_stored, 48 * (NT + 1))

        @block.tensor
        def _(pe):
            pe.wait_ge(weights, 16 * n_weights)

            def front(i, c, b):
                for m in range(2 * MI):
                    pe.wait_ge(in_read, i * 8 + m + 1)
                    for k in range(KD):
                        last = nc.tensor.matmul(in_bank[:, m % 4, :], w_in[:, k, m * P:(m + 1) * P],
                                                xnT[:, k, bass.ds(i * TW, TW)], start=(k == 0), stop=(k == KD - 1))
                    last.then_inc(in_ready, 1)

            def back(i, c, b):
                pe.wait_ge(u_ready, i * 4 + 8)
                pe.wait_ge(back_read, i * 7 + 7)
                for bank, lo, n in ((2, 0, RANK), (0, RANK, 2 * NS), (1, RANK + 2 * NS, 2 * NS)):
                    for m in range(MI):
                        last = nc.tensor.matmul(bk_bank[0:n, bank, :], w_x[:, m, lo:lo + n], u[:, c % 2, m, :],
                                                start=(m == 0), stop=(m == MI - 1))
                    last.then_inc(back_ready, 1)
                for m in range(MI):
                    pe.wait_ge(back_read, i * 7 + (8, 8, 11, 12)[m])
                    nc.tensor.matmul(bk_bank[:, (3, 2)[m % 2], :], w_dt[:, m * P:(m + 1) * P], dtr[:, :],
                                     start=True, stop=True).then_inc(back_ready, 1)

            def step(i, c, b, ahead1, ahead2):
                if ahead1:
                    front(*ahead1)
                back(i, c, b)

            front(0, 0, 0)
            over_tiles(pe, step)

        @block.scalar
        def _(act):
            act.sem_inc(in_read, 4)
            act.sem_inc(back_read, 7)
            act.sem_inc(u_ready, 4)
            for s in range(2):
                act.sem_inc(u_stored[s], 16)
                act.sem_inc(sz_stored[s], 16)
                act.sem_inc(bc_stored[s], 32)
            act.sem_inc(dparts_stored, 48)
            act.sem_inc(uparts_stored, 48)
            act.wait_ge(weights, 16 * n_weights)

            def front(i, c, b):
                act.wait_ge(xi_free, i + 1)
                for m in range(MI):
                    act.wait_ge(in_ready, i * 8 + m + 1)
                    nc.scalar.activation(xi[:, m, TAPS - 1:TAPS - 1 + TW], in_bank[:, m, :],
                                         ACT.Identity).then_inc(in_read, 1)
                act.wait_ge(sz_stored[c % 2], b * 32 + (c // 2) * 16 + 16)
                for m in range(MI):
                    act.wait_ge(in_ready, i * 8 + MI + m + 1)
                    nc.scalar.activation(sz[:, c % 2, m, :], in_bank[:, m, :], ACT.Silu).then_inc(in_read, 1)

            def middle(i, c, b):
                act.wait_ge(du_done, i + 1)
                act.wait_ge(u_stored[c % 2], b * 32 + (c // 2) * 16 + 16)
                for m in range(MI):
                    act.wait_ge(conv_done, i * 4 + m + 1)
                    nc.scalar.activation(u[:, c % 2, m, :], acc[:, m, :], ACT.Silu,
                                         bias=conv_b[:, m:m + 1]).then_inc(u_ready, 1)

            def step(i, c, b, ahead1, ahead2):
                if ahead1:
                    front(*ahead1)
                act.wait_ge(back_ready, i * 7 + 1)
                nc.scalar.activation(dtr[:, :], bk_bank[0:RANK, 2, :], ACT.Identity).then_inc(back_read, 1)
                act.wait_ge(bc_stored[c % 2], b * 64 + (c // 2) * 32 + 32)
                for k in range(2):
                    act.wait_ge(back_ready, i * 7 + 2 + k)
                    nc.scalar.activation(bc[:, c % 2, k, :], bk_bank[:, k, :], ACT.Identity).then_inc(back_read, 1)
                if ahead1:
                    middle(*ahead1)
                act.wait_ge(delta_done, i + 1)
                for m in range(MI):
                    act.wait_ge(back_ready, i * 7 + 4 + m)
                    nc.scalar.activation(v[:, m, :], bk_bank[:, (3, 2)[m % 2], :], ACT.Identity,
                                         bias=b_dt[:, m:m + 1]).then_inc(back_read, 1)
                act.wait_ge(back_read, i * 7 + 14)
                nc.scalar.activation(ex[:, :, :], v[:, :, :], ACT.Abs).then_inc(abs_done, 1)
                act.wait_ge(abs_done, i + 1)
                nc.scalar.activation(ex[:, :, :], ex[:, :, :], ACT.Exp, scale=-1.0).then_inc(exp_done, 1)
                act.wait_ge(w1_done, i + 1)
                nc.scalar.activation(lw[:, :, :], w1[:, :, :], ACT.Ln).then_inc(ln_done, 1)

            front(0, 0, 0)
            middle(0, 0, 0)
            over_tiles(act, step)

        @block.vector
        def _(dve):
            dve.sem_inc(delta_done, 1)
            nc.vector.memset(xi[:, :, 0:TAPS - 1], 0.0).then_inc(xi_free, 1)
            dve.wait_ge(weights, 16 * n_weights)

            def front(i, c, b):
                dve.wait_ge(xi_free, i + 1)
                for k in range(TAPS):
                    for m in range(MI):
                        tap, wk = xi[:, m, k:k + TW], conv_w[:, m, k:k + 1]
                        if k == 0:
                            dve.wait_ge(in_read, i * 8 + 5 + m)
                            dve.wait_ge(u_ready, i * 4 + m + 1)
                            nc.vector.tensor_scalar(acc[:, m, :], tap, wk, None, ALU.mult).then_inc(conv_step, 1)
                        else:
                            dve.wait_ge(conv_step, i * 12 + (k - 1) * 4 + m + 1)
                            nc.vector.scalar_tensor_tensor(
                                out=acc[:, m, :], in0=tap, scalar=wk, in1=acc[:, m, :], op0=ALU.mult,
                                op1=ALU.add).then_inc(conv_step if k < TAPS - 1 else conv_done, 1)
                dve.wait_ge(conv_done, i * 4 + 4)
                if c + 1 < TPB:
                    nc.vector.tensor_copy(xi[:, :, 0:TAPS - 1], xi[:, :, TW:TW + TAPS - 1]).then_inc(xi_free, 1)
                else:
                    nc.vector.memset(xi[:, :, 0:TAPS - 1], 0.0).then_inc(xi_free, 1)

            def softplus(i):
                dve.wait_ge(exp_done, i + 1)
                dve.wait_ge(d3_done, i + 1)
                nc.vector.tensor_scalar(w1[:, :, :], ex[:, :, :], 1.0, None, ALU.add).then_inc(w1_done, 1)
                dve.wait_ge(w1_done, i + 1)
                nc.vector.scalar_tensor_tensor(out=ex[:, :, :], in0=w1[:, :, :], scalar=1.0, in1=ex[:, :, :],
                                               op0=ALU.subtract, op1=ALU.subtract).then_inc(tail_done, 1)
                dve.wait_ge(tail_done, i + 1)
                dve.wait_ge(ln_done, i + 1)
                nc.vector.tensor_tensor(lw[:, :, :], lw[:, :, :], ex[:, :, :], ALU.subtract).then_inc(log_done, 1)
                dve.wait_ge(log_done, i + 1)
                nc.vector.scalar_tensor_tensor(out=lw[:, :, :], in0=v[:, :, :], scalar=0.0, in1=lw[:, :, :],
                                               op0=ALU.max, op1=ALU.add).then_inc(delta_done, 1)

            def split(i):
                for src, rest, parts, stored, first, whole, one, left, two in (
                        (lw, w1, dparts, dparts_stored, delta_done, i + 2, d1_done, dr_done, d2_done),
                        (du, du_rest, uparts, uparts_stored, du_done, i + 3, u1_done, ur_done, u2_done)):
                    dve.wait_ge(first, whole)
                    dve.wait_ge(stored, i * 48 + 48)
                    nc.vector.tensor_copy(parts[:, 0], src[:, :, :]).then_inc(one, 1)
                    dve.wait_ge(one, i + 1)
                    if rest is du_rest:
                        dve.wait_ge(u3_done, i + 1)
                    nc.vector.tensor_tensor(rest[:, :, :], src[:, :, :], parts[:, 0], ALU.subtract).then_inc(left, 1)
                    dve.wait_ge(left, i + 1)
                    nc.vector.tensor_copy(parts[:, 1], rest[:, :, :]).then_inc(two, 1)

            def step(i, c, b, ahead1, ahead2):
                softplus(i)
                if ahead2:
                    front(*ahead2)
                split(i)

            front(0, 0, 0)
            front(1, 1, 0)
            over_tiles(dve, step)

        @block.gpsimd
        def _(pool):
            pool.sem_inc(u3_done, 1)
            pool.sem_inc(d3_done, 1)
            pool.sem_inc(du_done, 2)

            def step(i, c, b, ahead1, ahead2):
                pool.wait_ge(delta_done, i + 2)
                nc.gpsimd.tensor_tensor(du[:, :, :], lw[:, :, :], u[:, c % 2], ALU.mult).then_inc(du_done, 1)
                pool.wait_ge(d2_done, i + 1)
                nc.gpsimd.tensor_tensor(dparts[:, 2], w1[:, :, :], dparts[:, 1], ALU.subtract).then_inc(d3_done, 1)
                pool.wait_ge(u2_done, i + 1)
                nc.gpsimd.tensor_tensor(uparts[:, 2], du_rest[:, :, :], uparts[:, 1], ALU.subtract).then_inc(u3_done, 1)

            over_tiles(pool, step)


def scan_stage(nc, d):
    with ExitStack() as ctx:
        def sb(name, shape, dt=F32):
            return ctx.enter_context(nc.sbuf_tensor(name, shape, dt))

        def sem(name):
            return ctx.enter_context(nc.semaphore(name))

        NC, ND = len(COPIED), len(DIRECT)
        copied_before = [sum(m in COPIED for m in range(n)) for n in range(2 * QUADS + 1)]
        direct_before = [n - copied_before[n] for n in range(2 * QUADS + 1)]
        assert NC % COPIES == 0 and DIRECT[0] >= 2 * WINDOW_QUAD
        NL = len(COMBOS) + 3 + 2

        H = [sb(f"s_h{s}", [P, PAIRS, SEG]) for s in range(2)]
        decay = sb("s_decay", [P, RING, 4, SEG])
        ducopy = sb("s_ducopy", [P, COPIES, 2, CH])
        dl = sb("s_dl", [P, 2, 8, CH], BF16)
        duo_in = sb("s_du", [96, 2, 4, CH], BF16)
        Bs = sb("s_b", [P, 2, CH])
        Cs = sb("s_c", [P, 2, CH])
        window = sb("s_window", [P, CH * WIN])
        a_w = sb("s_a", [P, PAIRS, P], BF16)
        sel = sb("s_sel", [96, 16, P], BF16)
        yout = sb("s_y", [P, 2, 512])
        a_bank = ctx.enter_context(nc.psum_tensor("s_abank", [P, 2, 4, CH], F32))
        u_bank = ctx.enter_context(nc.psum_tensor("s_ubank", [P, U_BANKS, 2, CH], F32))
        y_bank = ctx.enter_context(nc.psum_tensor("s_ybank", [P, 512], F32))

        loaded = [sem("loaded0"), sem("loaded1")]
        a_loaded = sem("a_w_loaded")
        sel_ready = sem("sel_ready")
        a_ready = sem("a_ready")
        exp_done = sem("decay_ready")
        u_ready = sem("spread_u_ready")
        u_copied = sem("u_copied")
        dbu_pool = sem("dbu_pool")
        dbu_dve = sem("dbu_dve")
        scan_done = sem("scan_done")
        carry_done = sem("carry_done")
        window_ready = sem("window_ready")
        y_ready = sem("y_ready")
        y_read = sem("y_read")
        y_stored = [sem("y_stored0"), sem("y_stored1")]

        block = ctx.enter_context(nc.Block())

        set_quads = [FIRST_C + s * (QUADS - FIRST_C) // SETS for s in range(SETS)]

        def over_chunks(eng, chunk, at_group=None, at_batch=None):
            with eng.Fori(0, NG) as g:
                if at_group:
                    at_group(g)
                with eng.Fori(0, BATCH) as b:
                    if at_batch:
                        at_batch(g, b)
                    with eng.Fori(0, CPB // UNROLL) as c:
                        for s in range(UNROLL):
                            chunk(g, b, (b * (CPB // UNROLL) + c) * UNROLL + s, s % 2)

        def number(g, i):
            return g * NB + i

        @block.sync
        def _(sp):
            def at_group(g):
                sp.wait_ge(u_ready, g * (NB * 2 * QUADS) + 4 * QUADS)
                sp.dma_start(a_w[:, :, :], d["a_image"][g]).then_inc(a_loaded, 16)

            def store(f, s):
                sp.wait_ge(y_read, f + 2)
                for ct in range(4):
                    dst = d["y"][f].rearrange("(e c r) k -> c r e k", c=4, r=WIN)[ct]
                    src = yout[32 * ct:32 * ct + WIN, s].rearrange("p (e k) -> p e k", k=64)
                    sp.dma_start(dst, src).then_inc(y_stored[s], 16)

            def chunk(g, b, i, s):
                f = number(g, i)
                sp.wait_ge(window_ready, f * 2 + 2)
                t = bass.ds(i * CH, CH)
                for c, (_, j) in enumerate(COMBOS):
                    src = d["dparts"][j, bass.ds(g * P, P), t].rearrange("(r s) t -> r s t", s=8)
                    sp.dma_start(dl[16 * c:16 * c + 16, s], src).then_inc(loaded[s], 16)
                for j in range(3):
                    src = d["uparts"][j, bass.ds(g * P, P), t].rearrange("(r s) t -> r s t", s=4)
                    sp.dma_start(duo_in[32 * j:32 * j + 32, s], src).then_inc(loaded[s], 16)
                sp.dma_start(Bs[:, s], d["B"][:, t]).then_inc(loaded[s], 16)
                sp.dma_start(Cs[:, s], d["C"][:, t]).then_inc(loaded[s], 16)
                store(f, s)

            over_chunks(sp, chunk, at_group)
            last = NG * NB
            store(last, 0)
            store(last + 1, 1)
            for s in range(2):
                sp.wait_ge(y_stored[s], 64 * (last // 2 + 2))

        @block.tensor
        def _(pe):
            pe.sem_inc(u_ready, 4 * QUADS)
            pe.wait_ge(sel_ready, 4)
            pe.wait_ge(y_read, 1)
            pe.sem_inc(y_ready, 1)

            def contract(f, e, s):
                if e == 0:
                    pe.wait_ge(scan_done, f * QUADS + QUADS)
                    pe.wait_ge(window_ready, f * 2 + 4)
                    pe.wait_ge(y_read, f + 2)
                col = (e // 2) * 64
                for tt in range(4 * (e % 2), 4 * (e % 2) + 4):
                    for ct in range(4):
                        t = (e // 2) * (4 * WSTEPS) + ct * WSTEPS + tt
                        last = nc.tensor.matmul(y_bank[32 * ct:32 * ct + WIN, col:col + 64],
                                                window[:, t * WIN:(t + 1) * WIN], H[s][:, :, 1 + t],
                                                start=(tt == 0), stop=(tt == WSTEPS - 1))
                if e == SETS - 1:
                    last.then_inc(y_ready, 1)

            def chunk(g, b, i, s):
                f = number(g, i)
                pe.wait_ge(a_loaded, g * 16 + 16)
                pe.wait_ge(loaded[s], (f - s) * (8 * NL) + 16 * NL)
                for q in range(QUADS):
                    pe.wait_ge(exp_done, f * QUADS + q + 1)
                    for k in range(4):
                        last = nc.tensor.matmul(a_bank[:, q % 2, k, :], a_w[:, 4 * q + k, :],
                                                dl[:, s, (4 * q + k) % 8, :], start=True, stop=True)
                    last.then_inc(a_ready, 1)
                    for n in (2 * q, 2 * q + 1):
                        users = [m for m in range(2 * QUADS) if m % U_BANKS == n % U_BANKS]
                        before, back = (n - U_BANKS, 0) if n >= U_BANKS else (users[-1], 1)
                        if before in COPIED:
                            pe.wait_ge(u_copied, (f + (1 - back)) * NC + copied_before[before + 1])
                        else:
                            pe.wait_ge(dbu_dve, (f + (1 - back)) * ND + direct_before[before + 1])
                        k = n % 2
                        nc.tensor.matmul(u_bank[:, n % U_BANKS], sel[:, q, :], duo_in[:, s, 2 * k:2 * k + 2, :],
                                         start=True, stop=True).then_inc(u_ready, 1)
                    for e in range(SETS):
                        if set_quads[e] == q:
                            contract(f, e, 1 - s)

            over_chunks(pe, chunk)
            for e in range(SETS):
                contract(NG * NB, e, 1)

        @block.scalar
        def _(act):
            act.sem_inc(exp_done, 2)
            act.sem_inc(u_copied, NC)
            for s in range(2):
                act.sem_inc(y_stored[s], 64)

            def take_y(f, s):
                act.wait_ge(y_stored[s], (f - s) * 32 + 64)
                act.wait_ge(y_ready, f + 1)
                nc.scalar.activation(yout[:, s], y_bank[:, :], ACT.Identity).then_inc(y_read, 1)

            def chunk(g, b, i, s):
                f = number(g, i)
                for q in range(QUADS):
                    act.wait_ge(a_ready, f * QUADS + q + 1)
                    act.wait_ge(scan_done, f * QUADS + (q + 1 - RING + QUADS))
                    nc.scalar.activation(decay[:, q % RING, :, 1:SEG], a_bank[:, q % 2], ACT.Exp).then_inc(exp_done, 1)
                    for n in (2 * q, 2 * q + 1):
                        if n not in COPIED:
                            continue
                        c = copied_before[n]
                        act.wait_ge(dbu_pool, f * NC + (NC + c - COPIES + 1))
                        act.wait_ge(u_ready, f * (2 * QUADS) + (4 * QUADS + n + 1))
                        nc.scalar.activation(ducopy[:, c % COPIES], u_bank[:, n % U_BANKS],
                                             ACT.Identity).then_inc(u_copied, 1)
                    if q == Y_QUAD:
                        take_y(f, s)

            over_chunks(act, chunk)
            take_y(NG * NB, 0)
            take_y(NG * NB + 1, 1)

        @block.vector
        def _(dve):
            dve.sem_inc(dbu_dve, ND)
            nc.vector.memset(y_bank[:, :], 0.0).then_inc(y_read, 1)
            nc.vector.memset(window[:, :], 0.0).then_inc(window_ready, 1)
            nc.vector.memset(Cs[:, 1], 0.0).then_inc(window_ready, 1)
            nc.vector.memset(decay[:, :, :, 0:1], 0.0).then_inc(carry_done, 1)
            nc.vector.memset(H[1][:, :, :], 0.0).then_inc(scan_done, QUADS)

            def at_batch(g, b):
                n = g * (NB + BATCH) + b * (CPB + 1)
                dve.wait_ge(carry_done, n + 1)
                nc.vector.memset(H[0][:, :, 0:1], 0.0).then_inc(carry_done, 1)

            def lay_window(f, s):
                dve.wait_ge(y_ready, f + 1)
                dve.wait_ge(window_ready, f * 2 + 2)
                for p in range(2):
                    w = window[64 * p:64 * p + 64, :]
                    dst = bass.AP(w.tensor, w.offset + p,
                                  [list(w.ap[0]), [WSTEPS * WIN, CH // WSTEPS], [WIN + 2, WSTEPS]])
                    src = Cs[64 * p:64 * p + 64, s, :].rearrange("p (a c) -> p a c", c=WSTEPS)
                    nc.vector.tensor_copy(dst, src).then_inc(window_ready, 1)

            def chunk(g, b, i, s):
                f = number(g, i)
                dve.wait_ge(loaded[s], (f - s) * (8 * NL) + 16 * NL)
                for q in range(QUADS + LAG):
                    if q == WINDOW_QUAD:
                        lay_window(f, 1 - s)
                    for n in (2 * q, 2 * q + 1):
                        if n in DIRECT:
                            dve.wait_ge(u_ready, f * (2 * QUADS) + (4 * QUADS + n + 1))
                            nc.vector.tensor_tensor(H[s][:, 2 * n:2 * n + 2, 1:SEG], u_bank[:, n % U_BANKS],
                                                    Bs[:, s:s + 1, :].broadcast_to([P, 2, CH]),
                                                    ALU.mult).then_inc(dbu_dve, 1)
                    r = q - LAG
                    if r < 0:
                        continue
                    if r == 0:
                        dve.wait_ge(carry_done, f + (g * BATCH + b) + 2)
                    dve.wait_ge(exp_done, f * QUADS + r + 3)
                    if copied_before[2 * r + 2] > copied_before[2 * r]:
                        dve.wait_ge(dbu_pool, f * NC + (NC + copied_before[2 * r + 2]))
                    if direct_before[2 * r + 2] > direct_before[2 * r]:
                        dve.wait_ge(dbu_dve, f * ND + (ND + direct_before[2 * r + 2]))
                    h = H[s][:, 4 * r:4 * r + 4, :].rearrange("p a t -> p (a t)")
                    nc.vector.tensor_tensor_scan(h, decay[:, r % RING].rearrange("p a t -> p (a t)"), h, 0.0,
                                                 ALU.mult, ALU.add).then_inc(scan_done, 1)
                dve.wait_ge(scan_done, f * QUADS + 2 * QUADS)
                nc.vector.tensor_copy(H[1 - s][:, :, 0:1], H[s][:, :, CH:SEG]).then_inc(carry_done, 1)

            over_chunks(dve, chunk, at_batch=at_batch)
            lay_window(NG * NB, 1)

        @block.gpsimd
        def _(pool):
            pool.sem_inc(dbu_pool, NC)
            nc.gpsimd.memset(sel[:, :, :], 0.0).then_inc(sel_ready, 1)
            pool.wait_ge(sel_ready, 1)
            v = sel[:, :, :].rearrange("p q (h n) -> p q h n", h=2)
            for j in range(3):
                pool.wait_ge(sel_ready, j + 1)
                nc.gpsimd.affine_select(out=v, in_=v, compare_op=ALU.not_equal, fill=1.0, base=-32 * j,
                                        pattern=[[-1, 16], [-16, 2], [0, NS]],
                                        channel_multiplier=1).then_inc(sel_ready, 1)

            def chunk(g, b, i, s):
                f = number(g, i)
                pool.wait_ge(loaded[s], (f - s) * (8 * NL) + 16 * NL)
                pool.wait_ge(y_ready, f + 1)
                for c, n in enumerate(COPIED):
                    pool.wait_ge(u_copied, f * NC + (NC + c + 1))
                    nc.gpsimd.tensor_tensor(H[s][:, 2 * n:2 * n + 2, 1:SEG], ducopy[:, c % COPIES],
                                            Bs[:, s:s + 1, :].broadcast_to([P, 2, CH]),
                                            ALU.mult).then_inc(dbu_pool, 1)

            over_chunks(pool, chunk)


def output_stage(nc, d):
    with ExitStack() as ctx:
        def sb(name, shape, dt=F32):
            return ctx.enter_context(nc.sbuf_tensor(name, shape, dt))

        def sem(name):
            return ctx.enter_context(nc.semaphore(name))

        raw = sb("o_raw", [P, 3, MH * DM], I32)
        wf = sb("o_wf", [P, 3, MH * DM])
        wg = sb("o_wg", [P, KD, HID])
        wu = sb("o_wu", [P, KD, HID])
        wd = sb("o_wd", [P, MH, DM])
        w_out = sb("o_w_out", [P, MI, DM])
        dskip = sb("o_dskip", [P, MI])
        half = sb("o_half", [P, SUB])
        spare = sb("o_spare", [P, 1])
        ident = sb("o_ident", [P, P])
        y = sb("o_y", [P, SUB, NG, P])
        u = sb("o_u", [P, MI, TW])
        sz = sb("o_sz", [P, MI, TW])
        yg = sb("o_yg", [P, MI, TW])
        res = sb("o_res", [P, SUB, DM])
        x1 = sb("o_x1", [P, 2, SUB, DM])
        xf = sb("o_xf", [P, SUB, DM])
        xfT = sb("o_xfT", [P, KD, TW])
        stats = sb("o_stats", [P, SUB, 6])
        mv = sb("o_mv", [P, SUB, 2])
        veps = sb("o_veps", [P, SUB])
        rstd = sb("o_rstd", [P, SUB])
        sg = sb("o_sg", [P, 2, TW])
        hid = sb("o_hid", [P, MH, TW])
        out = sb("o_out", [P, SUB, DM])
        tr = ctx.enter_context(nc.psum_tensor("o_tr", [P, 2, TW], F32))
        gu = ctx.enter_context(nc.psum_tensor("o_gu", [P, 2, 2, TW], F32))
        ob = ctx.enter_context(nc.psum_tensor("o_ob", [P, SUB, DM], F32))

        w_loaded = sem("w_loaded")
        consts = sem("o_consts")
        w_scaled = sem("w_scaled")
        w_turned = sem("w_turned")
        w_read = sem("w_read")
        y_loaded, u_loaded, sz_loaded = sem("y_loaded"), sem("u_loaded"), sem("sz_loaded")
        res_loaded = sem("res_loaded")
        tr_ready = sem("o_tr_ready")
        y_taken = sem("y_taken")
        xf_taken = sem("xf_taken")
        gated = sem("gated")
        proj_ready = sem("proj_ready")
        x1_done = sem("x1_done")
        stats_done, mv_done, veps_done = sem("o_stats_done"), sem("o_mv_done"), sem("o_veps_done")
        rstd_done = sem("o_rstd_done")
        xf_done = sem("xf_done")
        gu_ready = sem("gu_ready")
        silu_done = sem("silu_done")
        hid_done = sem("hid_done")
        down_ready = sem("down_ready")
        out_done = sem("out_done")
        out_stored = sem("out_stored")

        block = ctx.enter_context(nc.Block())
        n_turns = 3 * KD * MH

        def over_tiles(eng, first, second):
            for k in range(3):
                first(0, 0, k)

            def step(i, s):
                for k in range(3):
                    first(i + 1, 1 - s, k)
                    second(i, s, k)

            with eng.Fori(0, NT // 2 - 1) as j:
                for s in range(2):
                    step(j * 2 + s, s)
            step(NT - 2, 0)
            for k in range(3):
                second(NT - 1, 1, k, True)

        def nothing(i, s, k, last_tile=False):
            pass

        def turned(n):
            w, r = n // (KD * MH), n % (KD * MH)
            if w < 2:
                m, k = r // KD, r % KD
                return wf[:, w, m * DM + k * P:m * DM + (k + 1) * P], (wg, wu)[w][:, k, m * P:(m + 1) * P]
            k, m = r // MH, r % MH
            return wf[:, 2, k * HID + m * P:k * HID + (m + 1) * P], wd[:, m, k * P:(k + 1) * P]

        @block.sync
        def _(sp):
            for w, name in enumerate(("w_gate", "w_up")):
                sp.dma_start(raw[:, w].rearrange("p (m c) -> p m c", c=DM),
                             d[name].rearrange("(m p) c -> p m c", p=P)).then_inc(w_loaded, 16)
            sp.dma_start(raw[:, 2].rearrange("p (k h) -> p k h", h=HID),
                         d["w_down"].rearrange("(k p) h -> p k h", p=P)).then_inc(w_loaded, 16)
            sp.dma_start(w_out[:, :, :], d["W_out"].rearrange("(m p) n -> p m n", p=P)).then_inc(w_loaded, 16)
            sp.dma_start(dskip[:, :], d["D"].rearrange("(m p) -> p m", p=P), allow_slow_non_contiguous=True).then_inc(w_loaded, 16)

            yv = d["y"].rearrange("f (t h) k -> f t (h k)", h=2)

            def tile_of(dram, i):
                return dram.rearrange("(m p) t -> p m t", p=P)[:, :, bass.ds(i * TW, TW)]

            def first(i, s, k):
                if k != 0:
                    return
                sp.wait_ge(tr_ready, i * 6 + 2)
                for m in range(NG):
                    src = yv[bass.ds(i * 2 + (2 + m * NB), 2)].rearrange("f (s p) c -> p (f s) c", p=P)
                    sp.dma_start(y[:, :, m, :], src).then_inc(y_loaded, 16)
                sp.wait_ge(gated, i * 4 + 4)
                sp.dma_start(u[:, :, :], tile_of(d["u"], i)).then_inc(u_loaded, 16)
                sp.dma_start(sz[:, :, :], tile_of(d["sz"], i)).then_inc(sz_loaded, 16)
                sp.wait_ge(x1_done, i + 1)
                sp.dma_start(res[:, :, :], d["res"].rearrange("(i s p) c -> i p s c", s=SUB, p=P)[i]
                             ).then_inc(res_loaded, 16)

            def second(i, s, k, last_tile=False):
                if k != 2:
                    return
                sp.wait_ge(out_done, i + 3)
                sp.dma_start(d["out"].rearrange("(i s p) c -> i p s c", s=SUB, p=P)[i],
                             out[:, :, :]).then_inc(out_stored, 16)

            first(0, 0, 0)
            first(1, 1, 0)
            with sp.Fori(0, NT - 2) as i:
                first(i + 2, None, 0)
                second(i, None, 2)
            second(NT - 2, None, 2)
            second(NT - 1, None, 2)
            sp.wait_ge(out_stored, 16 * (NT + 1))

        @block.tensor
        def _(pe):
            pe.wait_ge(consts, 3)
            pe.wait_ge(w_scaled, 3)
            for n in range(n_turns):
                if n >= 2:
                    pe.wait_ge(w_read, n - 1)
                nc.tensor.transpose(tr[:, n % 2, 0:P], turned(n)[0], ident[:, :]).then_inc(w_turned, 1)
            pe.wait_ge(w_read, n_turns)
            pe.sem_inc(tr_ready, 4)
            pe.sem_inc(gu_ready, MH)
            pe.sem_inc(proj_ready, 1)
            pe.sem_inc(down_ready, 1)
            pe.wait_ge(w_loaded, 80)

            def first(i, s, k):
                if k == 0:
                    pe.wait_ge(y_loaded, i * 64 + 64)
                    for m in range(MI):
                        if m < 2:
                            pe.wait_ge(xf_taken, i * 2 + m + 1)
                        else:
                            pe.wait_ge(y_taken, i * 4 + m + 3)
                        for g in range(SUB):
                            last = nc.tensor.transpose(tr[:, m % 2, g * P:(g + 1) * P], y[:, g, m, :], ident[:, :])
                        last.then_inc(tr_ready, 1)
                if k == 1:
                    pe.wait_ge(gated, i * 4 + 8)
                    pe.wait_ge(out_done, i + 1)
                    pe.wait_ge(x1_done, i + 1)
                    for g in range(SUB):
                        for m in range(MI):
                            last = nc.tensor.matmul(ob[:, g, :], yg[:, m, g * P:(g + 1) * P], w_out[:, m, :],
                                                    start=(m == 0), stop=(m == MI - 1))
                    last.then_inc(proj_ready, 1)
                if k == 2:
                    pe.wait_ge(xf_done, i * 4 + 4)
                    pe.wait_ge(y_taken, i * 4 + 8)
                    for kk in range(KD):
                        for g in range(SUB):
                            last = nc.tensor.transpose(tr[:, kk, g * P:(g + 1) * P],
                                                       xf[:, g, kk * P:(kk + 1) * P], ident[:, :])
                        last.then_inc(tr_ready, 1)

            def second(i, s, k, last_tile=False):
                if k < 2:
                    if k == 0:
                        pe.wait_ge(xf_taken, i * 2 + 4)
                    for m in range(3 * k, 3 * k + 3):
                        pe.wait_ge(hid_done, i * 6 + m + 5)
                        for r, w in enumerate((wg, wu)):
                            for kk in range(KD):
                                last = nc.tensor.matmul(gu[:, m % 2, r, :], w[:, kk, m * P:(m + 1) * P],
                                                        xfT[:, kk, :], start=(kk == 0), stop=(kk == KD - 1))
                        last.then_inc(gu_ready, 1)
                else:
                    pe.wait_ge(hid_done, i * 6 + 12)
                    pe.wait_ge(x1_done, NT + 1 if last_tile else i + 3)
                    for g in range(SUB):
                        for m in range(MH):
                            last = nc.tensor.matmul(ob[:, g, :], hid[:, m, g * P:(g + 1) * P], wd[:, m, :],
                                                    start=(m == 0), stop=(m == MH - 1))
                    last.then_inc(down_ready, 1)

            over_tiles(pe, first, second)

        @block.scalar
        def _(act):
            for n in range(n_turns):
                act.wait_ge(w_turned, n + 1)
                nc.scalar.activation(turned(n)[1], tr[:, n % 2, 0:P], ACT.Identity).then_inc(w_read, 1)
            act.sem_inc(xf_taken, 2)
            act.sem_inc(out_stored, 16)

            def first(i, s, k):
                if k != 2:
                    return
                act.wait_ge(gu_ready, i * MH + MH)
                for kk in range(KD):
                    act.wait_ge(tr_ready, i * 6 + 9 + kk)
                    nc.scalar.activation(xfT[:, kk, :], tr[:, kk, :], ACT.Identity).then_inc(xf_taken, 1)

            def second(i, s, k, last_tile=False):
                if k == 2:
                    return
                for m in range(3 * k, 3 * k + 3):
                    act.wait_ge(gu_ready, i * MH + MH + m + 1)
                    act.wait_ge(hid_done, i * MH + m + 5)
                    nc.scalar.activation(sg[:, m % 2, :], gu[:, m % 2, 0, :], ACT.Silu).then_inc(silu_done, 1)

            over_tiles(act, first, second)

        @block.vector
        def _(dve):
            for w in range(3):
                dve.wait_ge(w_loaded, 80)
                nc.vector.tensor_scalar(wf[:, w], raw[:, w], WSCALE, None, ALU.mult).then_inc(w_scaled, 1)
            dve.sem_inc(y_taken, 4)
            dve.sem_inc(gated, 4)
            dve.sem_inc(x1_done, 1)
            dve.sem_inc(hid_done, MH)
            dve.sem_inc(out_done, 2)

            def first(i, s, k):
                if k == 0:
                    dve.wait_ge(u_loaded, i * 16 + 16)
                    dve.wait_ge(sz_loaded, i * 16 + 16)
                    dve.wait_ge(proj_ready, i + 1)
                    for m in range(MI):
                        dve.wait_ge(tr_ready, i * 6 + 5 + m)
                        nc.vector.scalar_tensor_tensor(out=yg[:, m, :], in0=u[:, m, :], scalar=dskip[:, m:m + 1],
                                                       in1=tr[:, m % 2, :], op0=ALU.mult,
                                                       op1=ALU.add).then_inc(y_taken, 1)
                    for m in range(MI):
                        dve.wait_ge(y_taken, i * 4 + 5 + m)
                        nc.vector.tensor_tensor(yg[:, m, :], yg[:, m, :], sz[:, m, :], ALU.mult).then_inc(gated, 1)
                if k == 1:
                    dve.wait_ge(res_loaded, i * 16 + 16)
                    dve.wait_ge(proj_ready, i + 2)
                    nc.vector.tensor_tensor(x1[:, s], ob[:, :, :], res[:, :, :], ALU.add).then_inc(x1_done, 1)
                    dve.wait_ge(x1_done, i + 2)
                    for g in range(SUB):
                        nc.vector.bn_stats(stats[:, g, :], x1[:, s, g, :]).then_inc(stats_done, 1)
                    dve.wait_ge(stats_done, i * 4 + 4)
                    nc.vector.memset(spare[:, 0:1], 0.0)
                    for g in range(SUB):
                        nc.vector.bn_aggr(mv[:, g, :], stats[:, g, :]).then_inc(mv_done, 1)
                    dve.wait_ge(mv_done, i * 4 + 4)
                    nc.vector.tensor_scalar(veps[:, :], mv[:, :, 1], EPS, None, ALU.add).then_inc(veps_done, 1)
                    dve.wait_ge(rstd_done, i + 1)
                    dve.wait_ge(tr_ready, i * 6 + 4)
                    for g in range(SUB):
                        nc.vector.tensor_scalar(xf[:, g, :], x1[:, s, g, :], mv[:, g, 0:1], rstd[:, g:g + 1],
                                                ALU.subtract, ALU.mult).then_inc(xf_done, 1)

            def second(i, s, k, last_tile=False):
                if k < 2:
                    if k == 0:
                        dve.wait_ge(down_ready, i + 1)
                    for m in range(3 * k, 3 * k + 3):
                        dve.wait_ge(silu_done, i * MH + m + 1)
                        nc.vector.tensor_tensor(hid[:, m, :], sg[:, m % 2, :], gu[:, m % 2, 1, :],
                                                ALU.mult).then_inc(hid_done, 1)
                else:
                    dve.wait_ge(down_ready, i + 2)
                    dve.wait_ge(out_stored, i * 16 + 16)
                    nc.vector.tensor_tensor(out[:, :, :], ob[:, :, :], x1[:, s], ALU.add).then_inc(out_done, 1)

            over_tiles(dve, first, second)

        @block.gpsimd
        def _(pool):
            nc.gpsimd.memset(half[:, :], -0.5).then_inc(consts, 1)
            nc.gpsimd.memset(ident[:, :], 0.0).then_inc(consts, 1)
            pool.wait_ge(consts, 2)
            nc.gpsimd.affine_select(out=ident[:, :], in_=ident[:, :], compare_op=ALU.not_equal, fill=1.0, base=0,
                                    pattern=[[-1, P]], channel_multiplier=1).then_inc(consts, 1)
            with pool.Fori(0, NT) as i:
                pool.wait_ge(veps_done, i + 1)
                nc.gpsimd.tensor_tensor(rstd[:, :], veps[:, :], half[:, :], ALU.pow).then_inc(rstd_done, 1)


def build(nc, d):
    d = dict(d)

    def scratch(name, shape, dt=F32):
        d[name] = nc.dram_tensor(f"scratch_{name}", shape, dt, kind="Internal").ap()

    scratch("res", [TOK, DM])
    scratch("u", [DI, TOK])
    scratch("sz", [DI, TOK])
    scratch("B", [P, TOK])
    scratch("C", [P, TOK])
    scratch("dparts", [3, DI, TOK], BF16)
    scratch("uparts", [3, DI, TOK], BF16)
    scratch("a_parts", [3, DI, NS], BF16)
    scratch("a_image", [NG, P, PAIRS * P], BF16)
    scratch("y", [2 + NG * NB, 2 * CH, 64])
    with nc.sbuf_tensor("xnT", [P, KD, TOK], F32) as xnT:
        decay_stage(nc, d)
        norm_stage(nc, d, xnT)
        project_stage(nc, d, xnT)
    scan_stage(nc, d)
    output_stage(nc, d)


_INS = ["x", "ln_w", "ln_b", "W_in", "conv_w", "conv_b", "W_xproj", "W_dt", "b_dt", "A_log", "D", "W_out"]
_FFN = ["w_gate", "w_up", "w_down"]


def kernel(**inputs):
    import numpy as np
    import concourse.bacc as bacc
    from concourse.bass_utils import run_bass_kernel_spmd

    nc = bacc.Bacc("TRN2", target_bir_lowering=False, num_devices=1, dynamic_dma_scratch_size=1024)
    arrays, d = {}, {}
    for name, key in [(n, f"L0_attn_{n}") for n in _INS] + [(n, f"L0_ffn_{n}") for n in _FFN]:
        a = np.ascontiguousarray(inputs[key])
        arrays[f"in_{name}"] = a
        d[name] = nc.dram_tensor(f"in_{name}", a.shape, mybir.dt.from_np(a.dtype), kind="ExternalInput").ap()
    d["x"] = d["x"].rearrange("b t c -> (b t) c")
    out = nc.dram_tensor("out", (BATCH, SEQ, DM), F32, kind="ExternalOutput").ap()
    d["out"] = out.rearrange("b t c -> (b t) c")
    build(nc, d)
    return run_bass_kernel_spmd(nc, [arrays], core_ids=[0]).results[0]["out"]
```

```python
from contextlib import ExitStack

import concourse.bass as bass
from concourse import mybir

ALU = mybir.AluOpType
ACT = mybir.ActivationFunctionType
F32 = mybir.dt.float32
BF16 = mybir.dt.bfloat16
I32 = mybir.dt.int32

P = 128
BATCH, SEQ, DM = 4, 2048, 256
DI, NS, RANK, TAPS = 512, 64, 16, 4
HID = 768
TOK = BATCH * SEQ
EPS = 1e-5
WSCALE = 1.0 / 127.0

TW = 512
NT = TOK // TW
TPB = SEQ // TW
SUB = TW // P
KD = DM // P
MI = DI // P
MH = HID // P
N_TURNS = 3 * KD * MH

CH = 256
NB = TOK // CH
CPB = SEQ // CH
NG = DI // P
PAIRS = P // 2
QUADS = PAIRS // 4
SEG = CH + 1
COMBOS = [(i, j) for j in range(3) for i in range(3) if i + j < 4]
WSTEPS = 8
WIN = 2 * WSTEPS
SETS = CH // 16
DIRECT = [4, 5, 8, 10, 13, 15, 18, 20, 23, 25, 28, 30]
COPIED = [n for n in range(2 * QUADS) if n not in DIRECT]
U_BANKS = 3
COPIES = 4
RING = 4
LAG = 2
FIRST_C = 3
WINDOW_QUAD = 2
Y_QUAD = 1


def turned_from(n):
    w, r = n // (KD * MH), n % (KD * MH)
    if w < 2:
        k, m = r // MH, r % MH
        return w, m * DM + k * P
    m, k = r // KD, r % KD
    return w, k * HID + m * P


def norm_stage(nc, d, xnT):
    with ExitStack() as ctx:
        def sb(name, shape, dt=F32):
            return ctx.enter_context(nc.sbuf_tensor(name, shape, dt))

        def sem(name):
            return ctx.enter_context(nc.semaphore(name))

        x = sb("n_x", [P, 4, SUB, DM])
        xa = sb("n_xa", [P, 4, SUB, DM])
        xn = sb("n_xn", [P, 2, SUB, DM])
        res = sb("n_res", [P, 2, SUB, DM])
        stats = sb("n_stats", [P, 2, 2, SUB, 6])
        mv = sb("n_mv", [P, 2, 2, SUB, 2])
        veps = sb("n_veps", [P, 2, 2, SUB])
        rstd = sb("n_rstd", [P, 2, 2, SUB])
        half = sb("n_half", [P, SUB])
        spare = sb("n_spare", [P, 1])
        ident = sb("n_ident", [P, P])
        lnw = sb("n_lnw", [P, KD])
        lnb = sb("n_lnb", [P, KD])
        a = sb("n_a", [P, MI, NS])
        a_split = sb("n_a_split", [P, 3, MI, NS], BF16)
        zeros = sb("n_zeros", [P, PAIRS * P // 2])
        raw = sb("n_raw", [P, 3, MH * DM], I32)
        w_bf = sb("n_w_bf", [P, 3, MH * DM], BF16)
        w_t = sb("n_w_t", [P, N_TURNS * P], BF16)
        ident_bf = sb("n_ident_bf", [P, P], BF16)
        turn_bank = ctx.enter_context(nc.psum_tensor("n_turn", [P, 2, 8 * P], BF16))
        tr = ctx.enter_context(nc.psum_tensor("n_tr", [P, 2, KD, TW], F32))

        x_loaded = [sem(f"x_loaded{q}") for q in range(4)]
        par_loaded = sem("par_loaded")
        consts = sem("consts")
        stats_done = sem("stats_done")
        mv_done = sem("mv_done")
        veps_done = sem("veps_done")
        rstd_done = sem("rstd_done")
        xa_done = sem("xa_done")
        xn_done = sem("xn_done")
        res_done = sem("res_done")
        res_stored = [sem("res_stored0"), sem("res_stored1")]
        tr_done = sem("tr_done")
        tr_read = sem("tr_read")

        a_loaded, a_exp, a_step = sem("a_loaded"), sem("a_exp"), sem("a_step")
        zeroed, image_zero = sem("zeroed"), sem("image_zero")
        parts_stored, placed = sem("parts_stored"), sem("placed")
        raw_loaded, w_cast, w_turned, w_read = sem("raw_loaded"), sem("w_cast"), sem("w_turned"), sem("w_read")
        w_t_stored = sem("w_t_stored")

        block = ctx.enter_context(nc.Block())

        def over_pairs(eng, pair):
            with eng.Fori(0, NT // 4) as jj:
                for r in range(2):
                    pair(jj * 2 + r, r)

        xv = d["x"].rearrange("(i s p) c -> i p s c", s=SUB, p=P)
        rv = d["res"].rearrange("(i s p) c -> i p s c", s=SUB, p=P)

        @block.sync
        def _(sp):
            sp.dma_start(a[:, :, :], d["A_log"].rearrange("(m p) n -> p m n", p=P)).then_inc(a_loaded, 16)
            sp.dma_start(lnw[:, :], d["ln_w"].rearrange("(k p) -> p k", p=P),
                         allow_slow_non_contiguous=True).then_inc(par_loaded, 16)
            sp.dma_start(lnb[:, :], d["ln_b"].rearrange("(k p) -> p k", p=P),
                         allow_slow_non_contiguous=True).then_inc(par_loaded, 16)
            for w, name in enumerate(("w_gate", "w_up")):
                sp.dma_start(raw[:, w].rearrange("p (m c) -> p m c", c=DM),
                             d[name].rearrange("(m p) c -> p m c", p=P)).then_inc(raw_loaded, 16)
            sp.dma_start(raw[:, 2].rearrange("p (k h) -> p k h", h=HID),
                         d["w_down"].rearrange("(k p) h -> p k h", p=P)).then_inc(raw_loaded, 16)

            row = PAIRS * P
            image = d["a_image"].tensor
            places = [(g, c, h) for g in range(NG) for c in range(len(COMBOS)) for h in range(2)]
            for i in range(NT):
                if i >= 4:
                    sp.wait_ge(res_done, i + 1)
                sp.dma_start(x[:, i % 4], xv[i]).then_inc(x_loaded[i % 4], 16)
                if i == 3:
                    sp.wait_ge(parts_stored, 48)
                    sp.wait_ge(image_zero, 16 * NG)
                if i < 3:
                    continue
                here = places[(i - 3) * len(places) // (NT - 3):(i - 2) * len(places) // (NT - 3)]
                for g, c, h in here:
                    dst = bass.AP(image, (g * P + c * 16 + 8 * h) * row + NS * h, [[row + 8 * P, 8], [P, 8], [1, NS]])
                    src = d["a_parts"][COMBOS[c][0], g * P + 64 * h:g * P + 64 * h + 64, :]
                    sp.dma_start(dst, src.rearrange("(k s) n -> k s n", k=8)).then_inc(placed, 16)
            sp.wait_ge(placed, 16 * len(places))

        @block.vector
        def _(dve):
            def layernorm(j, s, k, src):
                for g in range(SUB):
                    nc.vector.bn_stats(stats[:, s, k, g, :], src[:, g, :]).then_inc(stats_done, 1)
                n = j * 16 + k * 8 + s * 4
                dve.wait_ge(stats_done, n + 4)
                nc.vector.memset(spare[:, 0:1], 0.0)
                for g in range(SUB):
                    nc.vector.bn_aggr(mv[:, s, k, g, :], stats[:, s, k, g, :]).then_inc(mv_done, 1)
                dve.wait_ge(mv_done, n + 4)
                nc.vector.tensor_scalar(veps[:, s, k, :], mv[:, s, k, :, 1], EPS, None, ALU.add).then_inc(veps_done, 1)

            def scaled(j, s, k, src, dst, done):
                dve.wait_ge(rstd_done, j * 4 + k * 2 + s + 1)
                for g in range(SUB):
                    nc.vector.tensor_scalar(dst[:, g, :], src[:, g, :], mv[:, s, k, g, 0:1],
                                            rstd[:, s, k, g:g + 1], ALU.subtract, ALU.mult).then_inc(done, 1)

            count = [0]

            def a_steps(ins):
                count[0] += 1
                ins.then_inc(a_step, 1)
                dve.wait_ge(a_step, count[0])

            dve.wait_ge(a_exp, 1)
            a_steps(nc.vector.tensor_scalar(a[:, :, :], a[:, :, :], -1.0, -3.0e38, ALU.mult, ALU.max))
            a_steps(nc.vector.tensor_copy(a_split[:, 0], a[:, :, :]))
            a_steps(nc.vector.tensor_tensor(a[:, :, :], a[:, :, :], a_split[:, 0], ALU.subtract))
            a_steps(nc.vector.tensor_copy(a_split[:, 1], a[:, :, :]))
            a_steps(nc.vector.tensor_tensor(a_split[:, 2], a[:, :, :], a_split[:, 1], ALU.subtract))
            dve.wait_ge(consts, 3)
            nc.vector.tensor_copy(ident_bf[:, :], ident[:, :]).then_inc(w_cast, 1)
            dve.wait_ge(raw_loaded, 48)
            nc.vector.tensor_copy(w_bf[:, :, :], raw[:, :, :]).then_inc(w_cast, 1)

            def pair(j, r):
                for s in range(2):
                    dve.wait_ge(x_loaded[2 * r + s], (j - r) * 8 + 16)
                    layernorm(j, s, 0, x[:, 2 * r + s])
                for s in range(2):
                    dve.wait_ge(res_done, j * 2 + s + 1)
                    scaled(j, s, 0, x[:, 2 * r + s], xa[:, 2 * r + s], xa_done)
                for s in range(2):
                    dve.wait_ge(xa_done, j * 8 + s * 4 + 4)
                    layernorm(j, s, 1, xa[:, 2 * r + s])
                for s in range(2):
                    dve.wait_ge(tr_done, j * 2 + s + 1)
                    scaled(j, s, 1, xa[:, 2 * r + s], xn[:, s], xn_done)

            over_pairs(dve, pair)

        @block.gpsimd
        def _(pool):
            nc.gpsimd.memset(half[:, :], -0.5).then_inc(consts, 1)
            nc.gpsimd.memset(ident[:, :], 0.0).then_inc(consts, 1)
            pool.wait_ge(consts, 2)
            nc.gpsimd.affine_select(out=ident[:, :], in_=ident[:, :], compare_op=ALU.not_equal, fill=1.0, base=0,
                                    pattern=[[-1, P]], channel_multiplier=1).then_inc(consts, 1)
            nc.gpsimd.memset(zeros[:, :], 0.0).then_inc(zeroed, 1)
            pool.sem_inc(res_done, 4)

            def pair(j, r):
                for k in range(2):
                    for s in range(2):
                        pool.wait_ge(veps_done, j * 4 + k * 2 + s + 1)
                        nc.gpsimd.tensor_tensor(rstd[:, s, k, :], veps[:, s, k, :], half[:, :],
                                                ALU.pow).then_inc(rstd_done, 1)
                for s in range(2):
                    pool.wait_ge(xn_done, j * 8 + s * 4 + 4)
                    pool.wait_ge(res_stored[s], j * 16 + 16)
                    nc.gpsimd.tensor_tensor(res[:, s], x[:, 2 * r + s], xa[:, 2 * r + s],
                                            ALU.add).then_inc(res_done, 1)

            over_pairs(pool, pair)

        @block.tensor
        def _(pe):
            pe.wait_ge(w_cast, 2)
            for n in range(N_TURNS):
                if n % 4 == 0 and n >= 8:
                    pe.wait_ge(w_read, n // 4 - 1)
                w, at = turned_from(n)
                last = nc.tensor.transpose(turn_bank[:, n // 4 % 2, n % 4 * P:(n % 4 + 1) * P], w_bf[:, w, at:at + P],
                                           ident_bf[:, :])
                if n % 4 == 3:
                    last.then_inc(w_turned, 1)
            pe.wait_ge(consts, 3)
            pe.sem_inc(tr_done, 2)
            with pe.Fori(0, NT // 2) as j:
                for s in range(2):
                    pe.wait_ge(xn_done, j * 8 + s * 4 + 4)
                    pe.wait_ge(tr_read, j * 4 + s * 2 + 2)
                    for k in range(KD):
                        for g in range(SUB):
                            last = nc.tensor.transpose(tr[:, s, k, g * P:(g + 1) * P],
                                                       xn[:, s, g, k * P:(k + 1) * P], ident[:, :])
                    last.then_inc(tr_done, 1)

        @block.scalar
        def _(act):
            act.sem_inc(tr_read, 4)
            act.sem_inc(res_stored[0], 16)
            act.sem_inc(res_stored[1], 16)
            act.wait_ge(a_loaded, 16)
            nc.scalar.activation(a[:, :, :], a[:, :, :], ACT.Exp).then_inc(a_exp, 1)
            act.wait_ge(zeroed, 1)
            for g in range(NG):
                act.dma_start(d["a_image"][g], zeros[:, :].bitcast(BF16)).then_inc(image_zero, 16)
            act.wait_ge(a_step, 5)
            for k in range(3):
                act.dma_start(d["a_parts"][k].rearrange("(m p) n -> p m n", p=P),
                              a_split[:, k]).then_inc(parts_stored, 16)
            for q in range(N_TURNS // 4):
                act.wait_ge(w_turned, q + 1)
                nc.scalar.activation(w_t[:, q * 4 * P:(q + 1) * 4 * P], turn_bank[:, q % 2, 0:4 * P], ACT.Identity
                                     ).then_inc(w_read, 1)
            act.wait_ge(w_read, N_TURNS // 4)
            act.dma_start(d["w_turned"], w_t[:, :]).then_inc(w_t_stored, 16)
            act.wait_ge(par_loaded, 32)
            with act.Fori(0, NT // 2) as j:
                for s in range(2):
                    act.wait_ge(tr_done, j * 2 + s + 3)
                    for k in range(KD):
                        nc.scalar.activation(xnT[:, k, bass.ds((j * 2 + s) * TW, TW)], tr[:, s, k, :], ACT.Identity,
                                             bias=lnb[:, k:k + 1], scale=lnw[:, k:k + 1]).then_inc(tr_read, 1)
                    act.wait_ge(res_done, j * 2 + s + 5)
                    act.dma_start(rv[j * 2 + s], res[:, s]).then_inc(res_stored[s], 16)
            for s in range(2):
                act.wait_ge(res_stored[s], 16 * (NT // 2 + 1))
            act.wait_ge(w_t_stored, 16)


def project_stage(nc, d, xnT):
    with ExitStack() as ctx:
        def sb(name, shape, dt=F32):
            return ctx.enter_context(nc.sbuf_tensor(name, shape, dt))

        def sem(name):
            return ctx.enter_context(nc.semaphore(name))

        w_in = sb("p_w_in", [P, KD, 2 * DI])
        w_x = sb("p_w_x", [P, MI, RANK + 4 * NS])
        w_dt = sb("p_w_dt", [RANK, DI])
        conv_w = sb("p_conv_w", [P, MI, TAPS])
        conv_b = sb("p_conv_b", [P, MI])
        b_dt = sb("p_b_dt", [P, MI])
        xi = sb("p_xi", [P, MI, TAPS - 1 + TW])
        acc = sb("p_acc", [P, MI, TW])
        u = sb("p_u", [P, 2, MI, TW])
        sz = sb("p_sz", [P, 2, MI, TW])
        dtr = sb("p_dtr", [RANK, TW])
        bc = sb("p_bc", [P, 2, 2, TW])
        v = sb("p_v", [P, MI, TW])
        ex = sb("p_ex", [P, MI, TW])
        w1 = sb("p_w1", [P, MI, TW])
        lw = sb("p_lw", [P, MI, TW])
        du = sb("p_du", [P, MI, TW])
        du_rest = sb("p_du_rest", [P, MI, TW])
        dparts = sb("p_dparts", [P, 3, MI, TW], BF16)
        uparts = sb("p_uparts", [P, 3, MI, TW], BF16)
        in_bank = ctx.enter_context(nc.psum_tensor("p_in", [P, 4, TW], F32))
        bk_bank = ctx.enter_context(nc.psum_tensor("p_bk", [P, 4, TW], F32))

        weights = sem("weights")
        in_ready = sem("in_ready")
        in_read = sem("in_read")
        xi_free = sem("xi_free")
        conv_step = sem("conv_step")
        conv_done = sem("conv_done")
        u_ready = sem("u_ready")
        back_ready = sem("back_ready")
        back_read = sem("back_read")
        abs_done = sem("abs_done")
        exp_done = sem("exp_done")
        w1_done = sem("w1_done")
        ln_done = sem("ln_done")
        tail_done = sem("tail_done")
        log_done = sem("log_done")
        delta_done = sem("delta_done")
        du_done = sem("du_done")
        d1_done, dr_done, d2_done = sem("d1_done"), sem("dr_done"), sem("d2_done")
        d3_done = sem("d3_done")
        u1_done, ur_done, u2_done = sem("u1_done"), sem("ur_done"), sem("u2_done")
        u3_done = sem("u3_done")
        u_stored = [sem("u_stored0"), sem("u_stored1")]
        sz_stored = [sem("sz_stored0"), sem("sz_stored1")]
        bc_stored = [sem("bc_stored0"), sem("bc_stored1")]
        dparts_stored = sem("dparts_stored")
        uparts_stored = sem("uparts_stored")
        n_weights = 10

        block = ctx.enter_context(nc.Block())

        def over_tiles(eng, step):
            def batch(b, last):
                for c in range(TPB):
                    def at(c):
                        if c < TPB:
                            return b * TPB + c, c, b
                        return None if last else ((b + 1) * TPB + (c - TPB), c - TPB, b + 1)
                    step(b * TPB + c, c, b, at(c + 1), at(c + 2))

            with eng.Fori(0, BATCH - 1) as b:
                batch(b, False)
            batch(BATCH - 1, True)

        @block.sync
        def _(sp):
            wx = d["W_xproj"].rearrange("(m p) n -> p m n", p=P)
            sp.dma_start(w_in[:, :, :], d["W_in"].rearrange("(k p) n -> p k n", p=P)).then_inc(weights, 16)
            sp.dma_start(w_x[:, :, 0:RANK], wx[:, :, 0:RANK]).then_inc(weights, 16)
            for r in range(4):
                at, frm = RANK + NS * r, RANK + NS * (r // 2)
                sp.dma_start(w_x[:, :, at:at + NS], wx[:, :, frm:frm + NS]).then_inc(weights, 16)
            sp.dma_start(w_dt[:, :], d["W_dt"]).then_inc(weights, 16)
            sp.dma_start(conv_w[:, :, :], d["conv_w"].rearrange("(m p) o k -> p m (o k)", p=P)).then_inc(weights, 16)
            sp.dma_start(conv_b[:, :], d["conv_b"].rearrange("(m p) -> p m", p=P),
                         allow_slow_non_contiguous=True).then_inc(weights, 16)
            sp.dma_start(b_dt[:, :], d["b_dt"].rearrange("(m p) -> p m", p=P),
                         allow_slow_non_contiguous=True).then_inc(weights, 16)

            def tile_of(dram, i):
                return dram.rearrange("(m p) t -> p m t", p=P)[:, :, bass.ds(i * TW, TW)]

            def front_stores(i, c, b):
                sp.wait_ge(in_read, i * 8 + 12)
                sp.dma_start(tile_of(d["sz"], i), sz[:, c % 2]).then_inc(sz_stored[c % 2], 16)
                sp.wait_ge(u_ready, i * 4 + 8)
                sp.dma_start(tile_of(d["u"], i), u[:, c % 2]).then_inc(u_stored[c % 2], 16)

            def back_stores(i, c, b):
                sp.wait_ge(back_read, i * 7 + 10)
                sp.dma_start(d["B"][:, bass.ds(i * TW, TW)], bc[:, c % 2, 0, :]).then_inc(bc_stored[c % 2], 16)
                sp.wait_ge(d3_done, i + 2)
                sp.dma_start(d["C"][:, bass.ds(i * TW, TW)], bc[:, c % 2, 1, :]).then_inc(bc_stored[c % 2], 16)
                for k in range(3):
                    sp.dma_start(tile_of(d["dparts"][k], i), dparts[:, k]).then_inc(dparts_stored, 16)
                sp.wait_ge(u3_done, i + 2)
                for k in range(3):
                    sp.dma_start(tile_of(d["uparts"][k], i), uparts[:, k]).then_inc(uparts_stored, 16)

            def step(i, c, b, ahead1, ahead2):
                if ahead1:
                    front_stores(*ahead1)
                back_stores(i, c, b)

            front_stores(0, 0, 0)
            over_tiles(sp, step)
            for s in range(2):
                sp.wait_ge(u_stored[s], 16 * (NT // 2 + 1))
                sp.wait_ge(sz_stored[s], 16 * (NT // 2 + 1))
                sp.wait_ge(bc_stored[s], 32 * (NT // 2 + 1))
            sp.wait_ge(dparts_stored, 48 * (NT + 1))
            sp.wait_ge(uparts_stored, 48 * (NT + 1))

        @block.tensor
        def _(pe):
            pe.wait_ge(weights, 16 * n_weights)

            def front(i, c, b):
                for m in range(2 * MI):
                    pe.wait_ge(in_read, i * 8 + m + 1)
                    for k in range(KD):
                        last = nc.tensor.matmul(in_bank[:, m % 4, :], w_in[:, k, m * P:(m + 1) * P],
                                                xnT[:, k, bass.ds(i * TW, TW)], start=(k == 0), stop=(k == KD - 1))
                    last.then_inc(in_ready, 1)

            def back(i, c, b):
                pe.wait_ge(u_ready, i * 4 + 8)
                pe.wait_ge(back_read, i * 7 + 7)
                for bank, lo, n in ((2, 0, RANK), (0, RANK, 2 * NS), (1, RANK + 2 * NS, 2 * NS)):
                    for m in range(MI):
                        last = nc.tensor.matmul(bk_bank[0:n, bank, :], w_x[:, m, lo:lo + n], u[:, c % 2, m, :],
                                                start=(m == 0), stop=(m == MI - 1))
                    last.then_inc(back_ready, 1)
                for m in range(MI):
                    pe.wait_ge(back_read, i * 7 + (8, 8, 11, 12)[m])
                    nc.tensor.matmul(bk_bank[:, (3, 2)[m % 2], :], w_dt[:, m * P:(m + 1) * P], dtr[:, :],
                                     start=True, stop=True).then_inc(back_ready, 1)

            def step(i, c, b, ahead1, ahead2):
                if ahead1:
                    front(*ahead1)
                back(i, c, b)

            front(0, 0, 0)
            over_tiles(pe, step)

        @block.scalar
        def _(act):
            act.sem_inc(in_read, 4)
            act.sem_inc(back_read, 7)
            act.sem_inc(u_ready, 4)
            for s in range(2):
                act.sem_inc(u_stored[s], 16)
                act.sem_inc(sz_stored[s], 16)
                act.sem_inc(bc_stored[s], 32)
            act.sem_inc(dparts_stored, 48)
            act.sem_inc(uparts_stored, 48)
            act.wait_ge(weights, 16 * n_weights)

            def front(i, c, b):
                act.wait_ge(xi_free, i + 1)
                for m in range(MI):
                    act.wait_ge(in_ready, i * 8 + m + 1)
                    nc.scalar.activation(xi[:, m, TAPS - 1:TAPS - 1 + TW], in_bank[:, m, :],
                                         ACT.Identity).then_inc(in_read, 1)
                act.wait_ge(sz_stored[c % 2], b * 32 + (c // 2) * 16 + 16)
                for m in range(MI):
                    act.wait_ge(in_ready, i * 8 + MI + m + 1)
                    nc.scalar.activation(sz[:, c % 2, m, :], in_bank[:, m, :], ACT.Silu).then_inc(in_read, 1)

            def middle(i, c, b):
                act.wait_ge(du_done, i + 1)
                act.wait_ge(u_stored[c % 2], b * 32 + (c // 2) * 16 + 16)
                for m in range(MI):
                    act.wait_ge(conv_done, i * 4 + m + 1)
                    nc.scalar.activation(u[:, c % 2, m, :], acc[:, m, :], ACT.Silu,
                                         bias=conv_b[:, m:m + 1]).then_inc(u_ready, 1)

            def step(i, c, b, ahead1, ahead2):
                if ahead1:
                    front(*ahead1)
                act.wait_ge(back_ready, i * 7 + 1)
                nc.scalar.activation(dtr[:, :], bk_bank[0:RANK, 2, :], ACT.Identity).then_inc(back_read, 1)
                act.wait_ge(bc_stored[c % 2], b * 64 + (c // 2) * 32 + 32)
                for k in range(2):
                    act.wait_ge(back_ready, i * 7 + 2 + k)
                    nc.scalar.activation(bc[:, c % 2, k, :], bk_bank[:, k, :], ACT.Identity).then_inc(back_read, 1)
                if ahead1:
                    middle(*ahead1)
                act.wait_ge(delta_done, i + 1)
                for m in range(MI):
                    act.wait_ge(back_ready, i * 7 + 4 + m)
                    nc.scalar.activation(v[:, m, :], bk_bank[:, (3, 2)[m % 2], :], ACT.Identity,
                                         bias=b_dt[:, m:m + 1]).then_inc(back_read, 1)
                act.wait_ge(back_read, i * 7 + 14)
                nc.scalar.activation(ex[:, :, :], v[:, :, :], ACT.Abs).then_inc(abs_done, 1)
                act.wait_ge(abs_done, i + 1)
                nc.scalar.activation(ex[:, :, :], ex[:, :, :], ACT.Exp, scale=-1.0).then_inc(exp_done, 1)
                act.wait_ge(w1_done, i + 1)
                nc.scalar.activation(lw[:, :, :], w1[:, :, :], ACT.Ln).then_inc(ln_done, 1)

            front(0, 0, 0)
            middle(0, 0, 0)
            over_tiles(act, step)

        @block.vector
        def _(dve):
            dve.sem_inc(delta_done, 1)
            nc.vector.memset(xi[:, :, 0:TAPS - 1], 0.0).then_inc(xi_free, 1)
            dve.wait_ge(weights, 16 * n_weights)

            def front(i, c, b):
                dve.wait_ge(xi_free, i + 1)
                for k in range(TAPS):
                    for m in range(MI):
                        tap, wk = xi[:, m, k:k + TW], conv_w[:, m, k:k + 1]
                        if k == 0:
                            dve.wait_ge(in_read, i * 8 + 5 + m)
                            dve.wait_ge(u_ready, i * 4 + m + 1)
                            nc.vector.tensor_scalar(acc[:, m, :], tap, wk, None, ALU.mult).then_inc(conv_step, 1)
                        else:
                            dve.wait_ge(conv_step, i * 12 + (k - 1) * 4 + m + 1)
                            nc.vector.scalar_tensor_tensor(
                                out=acc[:, m, :], in0=tap, scalar=wk, in1=acc[:, m, :], op0=ALU.mult,
                                op1=ALU.add).then_inc(conv_step if k < TAPS - 1 else conv_done, 1)
                dve.wait_ge(conv_done, i * 4 + 4)
                if c + 1 < TPB:
                    nc.vector.tensor_copy(xi[:, :, 0:TAPS - 1], xi[:, :, TW:TW + TAPS - 1]).then_inc(xi_free, 1)
                else:
                    nc.vector.memset(xi[:, :, 0:TAPS - 1], 0.0).then_inc(xi_free, 1)

            def softplus(i):
                dve.wait_ge(exp_done, i + 1)
                dve.wait_ge(d3_done, i + 1)
                nc.vector.tensor_scalar(w1[:, :, :], ex[:, :, :], 1.0, None, ALU.add).then_inc(w1_done, 1)
                dve.wait_ge(w1_done, i + 1)
                nc.vector.scalar_tensor_tensor(out=ex[:, :, :], in0=w1[:, :, :], scalar=1.0, in1=ex[:, :, :],
                                               op0=ALU.subtract, op1=ALU.subtract).then_inc(tail_done, 1)
                dve.wait_ge(tail_done, i + 1)
                dve.wait_ge(ln_done, i + 1)
                nc.vector.tensor_tensor(lw[:, :, :], lw[:, :, :], ex[:, :, :], ALU.subtract).then_inc(log_done, 1)
                dve.wait_ge(log_done, i + 1)
                nc.vector.scalar_tensor_tensor(out=lw[:, :, :], in0=v[:, :, :], scalar=0.0, in1=lw[:, :, :],
                                               op0=ALU.max, op1=ALU.add).then_inc(delta_done, 1)

            def split(i):
                for src, rest, parts, stored, first, whole, one, left, two in (
                        (lw, w1, dparts, dparts_stored, delta_done, i + 2, d1_done, dr_done, d2_done),
                        (du, du_rest, uparts, uparts_stored, du_done, i + 3, u1_done, ur_done, u2_done)):
                    dve.wait_ge(first, whole)
                    dve.wait_ge(stored, i * 48 + 48)
                    nc.vector.tensor_copy(parts[:, 0], src[:, :, :]).then_inc(one, 1)
                    dve.wait_ge(one, i + 1)
                    if rest is du_rest:
                        dve.wait_ge(u3_done, i + 1)
                    nc.vector.tensor_tensor(rest[:, :, :], src[:, :, :], parts[:, 0], ALU.subtract).then_inc(left, 1)
                    dve.wait_ge(left, i + 1)
                    nc.vector.tensor_copy(parts[:, 1], rest[:, :, :]).then_inc(two, 1)

            def step(i, c, b, ahead1, ahead2):
                softplus(i)
                if ahead2:
                    front(*ahead2)
                split(i)

            front(0, 0, 0)
            front(1, 1, 0)
            over_tiles(dve, step)

        @block.gpsimd
        def _(pool):
            pool.sem_inc(u3_done, 1)
            pool.sem_inc(d3_done, 1)
            pool.sem_inc(du_done, 2)

            def step(i, c, b, ahead1, ahead2):
                pool.wait_ge(delta_done, i + 2)
                nc.gpsimd.tensor_tensor(du[:, :, :], lw[:, :, :], u[:, c % 2], ALU.mult).then_inc(du_done, 1)
                pool.wait_ge(d2_done, i + 1)
                nc.gpsimd.tensor_tensor(dparts[:, 2], w1[:, :, :], dparts[:, 1], ALU.subtract).then_inc(d3_done, 1)
                pool.wait_ge(u2_done, i + 1)
                nc.gpsimd.tensor_tensor(uparts[:, 2], du_rest[:, :, :], uparts[:, 1], ALU.subtract).then_inc(u3_done, 1)

            over_tiles(pool, step)


def scan_stage(nc, d):
    with ExitStack() as ctx:
        def sb(name, shape, dt=F32):
            return ctx.enter_context(nc.sbuf_tensor(name, shape, dt))

        def sem(name):
            return ctx.enter_context(nc.semaphore(name))

        NC, ND = len(COPIED), len(DIRECT)
        copied_before = [sum(m in COPIED for m in range(n)) for n in range(2 * QUADS + 1)]
        direct_before = [n - copied_before[n] for n in range(2 * QUADS + 1)]
        assert NC % COPIES == 0 and DIRECT[0] >= 2 * WINDOW_QUAD
        NL = len(COMBOS) + 3 + 2

        H = [sb(f"s_h{s}", [P, PAIRS, SEG]) for s in range(2)]
        decay = sb("s_decay", [P, RING, 4, SEG])
        ducopy = sb("s_ducopy", [P, COPIES, 2, CH])
        dl = sb("s_dl", [P, 2, 8, CH], BF16)
        duo_in = sb("s_du", [96, 2, 4, CH], BF16)
        Bs = sb("s_b", [P, 2, CH])
        Cs = sb("s_c", [P, 2, CH])
        window = sb("s_window", [P, CH * WIN])
        a_w = sb("s_a", [P, PAIRS, P], BF16)
        sel = sb("s_sel", [96, 16, P], BF16)
        yout = sb("s_y", [P, 2, 512])
        a_bank = ctx.enter_context(nc.psum_tensor("s_abank", [P, 2, 4, CH], F32))
        u_bank = ctx.enter_context(nc.psum_tensor("s_ubank", [P, U_BANKS, 2, CH], F32))
        y_bank = ctx.enter_context(nc.psum_tensor("s_ybank", [P, 512], F32))

        loaded = [sem("loaded0"), sem("loaded1")]
        a_loaded = sem("a_w_loaded")
        sel_ready = sem("sel_ready")
        a_ready = sem("a_ready")
        exp_done = sem("decay_ready")
        u_ready = sem("spread_u_ready")
        u_copied = sem("u_copied")
        dbu_pool = sem("dbu_pool")
        dbu_dve = sem("dbu_dve")
        scan_done = sem("scan_done")
        carry_done = sem("carry_done")
        window_ready = sem("window_ready")
        y_ready = sem("y_ready")
        y_read = sem("y_read")
        y_stored = [sem("y_stored0"), sem("y_stored1")]

        block = ctx.enter_context(nc.Block())

        set_quads = [FIRST_C + (e * (QUADS - FIRST_C) + SETS // 2) // SETS for e in range(SETS)]

        def over_chunks(eng, chunk, at_group=None, at_batch=None):
            with eng.Fori(0, NG) as g:
                if at_group:
                    at_group(g)
                with eng.Fori(0, BATCH) as b:
                    if at_batch:
                        at_batch(g, b)
                    for c in range(CPB):
                        chunk(g, b, b * CPB + c, c % 2)

        def number(g, i):
            return g * NB + i

        @block.sync
        def _(sp):
            def at_group(g):
                sp.wait_ge(u_ready, g * (NB * 2 * QUADS) + 4 * QUADS)
                sp.dma_start(a_w[:, :, :], d["a_image"][g]).then_inc(a_loaded, 16)

            def store(f, s):
                sp.wait_ge(y_read, f + 2)
                for ct in range(4):
                    dst = d["y"][f].rearrange("(e c r) k -> c r e k", c=4, r=WIN)[ct]
                    src = yout[32 * ct:32 * ct + WIN, s].rearrange("p (e k) -> p e k", k=64)
                    sp.dma_start(dst, src).then_inc(y_stored[s], 16)

            def chunk(g, b, i, s):
                f = number(g, i)
                sp.wait_ge(window_ready, f * 2 + 2)
                t = bass.ds(i * CH, CH)
                for c, (_, j) in enumerate(COMBOS):
                    src = d["dparts"][j, bass.ds(g * P, P), t].rearrange("(r s) t -> r s t", s=8)
                    sp.dma_start(dl[16 * c:16 * c + 16, s], src).then_inc(loaded[s], 16)
                for j in range(3):
                    src = d["uparts"][j, bass.ds(g * P, P), t].rearrange("(r s) t -> r s t", s=4)
                    sp.dma_start(duo_in[32 * j:32 * j + 32, s], src).then_inc(loaded[s], 16)
                sp.dma_start(Bs[:, s], d["B"][:, t]).then_inc(loaded[s], 16)
                sp.dma_start(Cs[:, s], d["C"][:, t]).then_inc(loaded[s], 16)
                store(f, s)

            over_chunks(sp, chunk, at_group)
            last = NG * NB
            store(last, 0)
            store(last + 1, 1)
            for s in range(2):
                sp.wait_ge(y_stored[s], 64 * (last // 2 + 2))

        @block.tensor
        def _(pe):
            pe.sem_inc(u_ready, 4 * QUADS)
            pe.wait_ge(sel_ready, 4)
            pe.wait_ge(y_read, 1)
            pe.sem_inc(y_ready, 1)

            def contract(f, e, s):
                if e == 0:
                    pe.wait_ge(scan_done, f * QUADS + QUADS)
                    pe.wait_ge(window_ready, f * 2 + 4)
                    pe.wait_ge(y_read, f + 2)
                col = (e // 2) * 64
                for tt in range(4 * (e % 2), 4 * (e % 2) + 4):
                    for ct in range(4):
                        t = (e // 2) * (4 * WSTEPS) + ct * WSTEPS + tt
                        last = nc.tensor.matmul(y_bank[32 * ct:32 * ct + WIN, col:col + 64],
                                                window[:, t * WIN:(t + 1) * WIN], H[s][:, :, 1 + t],
                                                start=(tt == 0), stop=(tt == WSTEPS - 1))
                if e == SETS - 1:
                    last.then_inc(y_ready, 1)

            def chunk(g, b, i, s):
                f = number(g, i)
                pe.wait_ge(a_loaded, g * 16 + 16)
                pe.wait_ge(loaded[s], (f - s) * (8 * NL) + 16 * NL)
                for q in range(QUADS):
                    pe.wait_ge(exp_done, f * QUADS + q + 1)
                    for k in range(4):
                        last = nc.tensor.matmul(a_bank[:, q % 2, k, :], a_w[:, 4 * q + k, :],
                                                dl[:, s, (4 * q + k) % 8, :], start=True, stop=True)
                    last.then_inc(a_ready, 1)
                    for e in range(SETS):
                        if set_quads[e] == q:
                            contract(f, e, 1 - s)
                    for n in (2 * q, 2 * q + 1):
                        users = [m for m in range(2 * QUADS) if m % U_BANKS == n % U_BANKS]
                        before, back = (n - U_BANKS, 0) if n >= U_BANKS else (users[-1], 1)
                        if before in COPIED:
                            pe.wait_ge(u_copied, (f + (1 - back)) * NC + copied_before[before + 1])
                        else:
                            pe.wait_ge(dbu_dve, (f + (1 - back)) * ND + direct_before[before + 1])
                        k = n % 2
                        nc.tensor.matmul(u_bank[:, n % U_BANKS], sel[:, q, :], duo_in[:, s, 2 * k:2 * k + 2, :],
                                         start=True, stop=True).then_inc(u_ready, 1)

            over_chunks(pe, chunk)
            for e in range(SETS):
                contract(NG * NB, e, 1)

        @block.scalar
        def _(act):
            act.sem_inc(exp_done, 2)
            act.sem_inc(u_copied, NC)
            for s in range(2):
                act.sem_inc(y_stored[s], 64)

            def take_y(f, s):
                act.wait_ge(y_stored[s], (f - s) * 32 + 64)
                act.wait_ge(y_ready, f + 1)
                nc.scalar.activation(yout[:, s], y_bank[:, :], ACT.Identity).then_inc(y_read, 1)

            def chunk(g, b, i, s):
                f = number(g, i)
                for q in range(QUADS):
                    act.wait_ge(a_ready, f * QUADS + q + 1)
                    act.wait_ge(scan_done, f * QUADS + (q + 1 - RING + QUADS))
                    nc.scalar.activation(decay[:, q % RING, :, 1:SEG], a_bank[:, q % 2], ACT.Exp).then_inc(exp_done, 1)
                    for n in (2 * q, 2 * q + 1):
                        if n not in COPIED:
                            continue
                        c = copied_before[n]
                        act.wait_ge(dbu_pool, f * NC + (NC + c - COPIES + 1))
                        act.wait_ge(u_ready, f * (2 * QUADS) + (4 * QUADS + n + 1))
                        nc.scalar.activation(ducopy[:, c % COPIES], u_bank[:, n % U_BANKS],
                                             ACT.Identity).then_inc(u_copied, 1)
                    if q == Y_QUAD:
                        take_y(f, s)

            over_chunks(act, chunk)
            take_y(NG * NB, 0)
            take_y(NG * NB + 1, 1)

        @block.vector
        def _(dve):
            dve.sem_inc(dbu_dve, ND)
            nc.vector.memset(y_bank[:, :], 0.0).then_inc(y_read, 1)
            nc.vector.memset(window[:, :], 0.0).then_inc(window_ready, 1)
            nc.vector.memset(Cs[:, 1], 0.0).then_inc(window_ready, 1)
            nc.vector.memset(decay[:, :, :, 0:1], 0.0).then_inc(carry_done, 1)
            nc.vector.memset(H[1][:, :, :], 0.0).then_inc(scan_done, QUADS)

            def at_batch(g, b):
                n = g * (NB + BATCH) + b * (CPB + 1)
                dve.wait_ge(carry_done, n + 1)
                nc.vector.memset(H[0][:, :, 0:1], 0.0).then_inc(carry_done, 1)

            def lay_window(f, s):
                dve.wait_ge(y_ready, f + 1)
                dve.wait_ge(window_ready, f * 2 + 2)
                for p in range(2):
                    w = window[64 * p:64 * p + 64, :]
                    dst = bass.AP(w.tensor, w.offset + p,
                                  [list(w.ap[0]), [WSTEPS * WIN, CH // WSTEPS], [WIN + 2, WSTEPS]])
                    src = Cs[64 * p:64 * p + 64, s, :].rearrange("p (a c) -> p a c", c=WSTEPS)
                    nc.vector.tensor_copy(dst, src).then_inc(window_ready, 1)

            def chunk(g, b, i, s):
                f = number(g, i)
                dve.wait_ge(loaded[s], (f - s) * (8 * NL) + 16 * NL)
                for q in range(QUADS + LAG):
                    if q == WINDOW_QUAD:
                        lay_window(f, 1 - s)
                    for n in (2 * q, 2 * q + 1):
                        if n in DIRECT:
                            dve.wait_ge(u_ready, f * (2 * QUADS) + (4 * QUADS + n + 1))
                            nc.vector.tensor_tensor(H[s][:, 2 * n:2 * n + 2, 1:SEG], u_bank[:, n % U_BANKS],
                                                    Bs[:, s:s + 1, :].broadcast_to([P, 2, CH]),
                                                    ALU.mult).then_inc(dbu_dve, 1)
                    r = q - LAG
                    if r < 0:
                        continue
                    if r == 0:
                        dve.wait_ge(carry_done, f + (g * BATCH + b) + 2)
                    dve.wait_ge(exp_done, f * QUADS + r + 3)
                    if copied_before[2 * r + 2] > copied_before[2 * r]:
                        dve.wait_ge(dbu_pool, f * NC + (NC + copied_before[2 * r + 2]))
                    if direct_before[2 * r + 2] > direct_before[2 * r]:
                        dve.wait_ge(dbu_dve, f * ND + (ND + direct_before[2 * r + 2]))
                    h = H[s][:, 4 * r:4 * r + 4, :].rearrange("p a t -> p (a t)")
                    nc.vector.tensor_tensor_scan(h, decay[:, r % RING].rearrange("p a t -> p (a t)"), h, 0.0,
                                                 ALU.mult, ALU.add).then_inc(scan_done, 1)
                dve.wait_ge(scan_done, f * QUADS + 2 * QUADS)
                nc.vector.tensor_copy(H[1 - s][:, :, 0:1], H[s][:, :, CH:SEG]).then_inc(carry_done, 1)

            over_chunks(dve, chunk, at_batch=at_batch)
            lay_window(NG * NB, 1)

        @block.gpsimd
        def _(pool):
            pool.sem_inc(dbu_pool, NC)
            nc.gpsimd.memset(sel[:, :, :], 0.0).then_inc(sel_ready, 1)
            pool.wait_ge(sel_ready, 1)
            v = sel[:, :, :].rearrange("p q (h n) -> p q h n", h=2)
            for j in range(3):
                pool.wait_ge(sel_ready, j + 1)
                nc.gpsimd.affine_select(out=v, in_=v, compare_op=ALU.not_equal, fill=1.0, base=-32 * j,
                                        pattern=[[-1, 16], [-16, 2], [0, NS]],
                                        channel_multiplier=1).then_inc(sel_ready, 1)

            def chunk(g, b, i, s):
                f = number(g, i)
                pool.wait_ge(loaded[s], (f - s) * (8 * NL) + 16 * NL)
                pool.wait_ge(y_ready, f + 1)
                for c, n in enumerate(COPIED):
                    pool.wait_ge(u_copied, f * NC + (NC + c + 1))
                    nc.gpsimd.tensor_tensor(H[s][:, 2 * n:2 * n + 2, 1:SEG], ducopy[:, c % COPIES],
                                            Bs[:, s:s + 1, :].broadcast_to([P, 2, CH]),
                                            ALU.mult).then_inc(dbu_pool, 1)

            over_chunks(pool, chunk)


def output_stage(nc, d):
    with ExitStack() as ctx:
        def sb(name, shape, dt=F32):
            return ctx.enter_context(nc.sbuf_tensor(name, shape, dt))

        def sem(name):
            return ctx.enter_context(nc.semaphore(name))

        wgu = sb("o_wgu", [P, 2, KD, HID], BF16)
        wd_bf = sb("o_wd_bf", [P, MH, DM], BF16)
        wd = sb("o_wd", [P, MH, DM])
        w_out = sb("o_w_out", [P, MI, DM])
        dskip = sb("o_dskip", [P, MI])
        half = sb("o_half", [P, SUB])
        spare = sb("o_spare", [P, 1])
        ident = sb("o_ident", [P, P])
        y = sb("o_y", [P, SUB, NG, P])
        u = sb("o_u", [P, MI, TW])
        sz = sb("o_sz", [P, MI, TW])
        yg = sb("o_yg", [P, MI, TW])
        res = sb("o_res", [P, SUB, DM])
        x1 = sb("o_x1", [P, 2, SUB, DM])
        xf = sb("o_xf", [P, SUB, DM])
        xrest = sb("o_xrest", [P, KD, TW])
        xparts = sb("o_xparts", [P, 3, KD, TW], BF16)
        stats = sb("o_stats", [P, SUB, 6])
        mv = sb("o_mv", [P, SUB, 2])
        veps = sb("o_veps", [P, SUB])
        rstd = sb("o_rstd", [P, SUB])
        sg = sb("o_sg", [P, 2, TW])
        hid = sb("o_hid", [P, MH, TW])
        out = sb("o_out", [P, SUB, DM])
        tr = ctx.enter_context(nc.psum_tensor("o_tr", [P, 2, TW], F32))
        gu = ctx.enter_context(nc.psum_tensor("o_gu", [P, 2, 2, TW], F32))
        ob = ctx.enter_context(nc.psum_tensor("o_ob", [P, SUB, DM], F32))

        w_loaded = sem("w_loaded")
        consts = sem("o_consts")
        w_wide = sem("w_wide")
        y_loaded, u_loaded, sz_loaded = sem("y_loaded"), sem("u_loaded"), sem("sz_loaded")
        res_loaded = sem("res_loaded")
        tr_ready = sem("o_tr_ready")
        y_taken = sem("y_taken")
        xpart1 = sem("xpart1")
        xrest_done = sem("xrest_done")
        xpart2 = sem("xpart2")
        xpart3 = sem("xpart3")
        gated = sem("gated")
        proj_ready = sem("proj_ready")
        x1_done = sem("x1_done")
        stats_done, mv_done, veps_done = sem("o_stats_done"), sem("o_mv_done"), sem("o_veps_done")
        rstd_done = sem("o_rstd_done")
        xf_done = sem("xf_done")
        gu_ready = sem("gu_ready")
        silu_done = sem("silu_done")
        hid_done = sem("hid_done")
        down_ready = sem("down_ready")
        out_done = sem("out_done")
        out_stored = sem("out_stored")

        block = ctx.enter_context(nc.Block())

        def over_tiles(eng, first, second):
            for k in range(3):
                first(0, 0, k)

            def step(i, s):
                for k in range(3):
                    first(i + 1, 1 - s, k)
                    second(i, s, k)

            with eng.Fori(0, NT // 2 - 1) as j:
                for s in range(2):
                    step(j * 2 + s, s)
            step(NT - 2, 0)
            for k in range(3):
                second(NT - 1, 1, k, True)

        @block.sync
        def _(sp):
            yv = d["y"].rearrange("f (t h) k -> f t (h k)", h=2)

            def tile_of(dram, i):
                return dram.rearrange("(m p) t -> p m t", p=P)[:, :, bass.ds(i * TW, TW)]

            def load(i):
                sp.wait_ge(tr_ready, i * 6 + 2)
                for m in range(NG):
                    src = yv[bass.ds(i * 2 + (2 + m * NB), 2)].rearrange("f (s p) c -> p (f s) c", p=P)
                    sp.dma_start(y[:, :, m, :], src).then_inc(y_loaded, 16)
                sp.wait_ge(gated, i * 4 + 4)
                sp.dma_start(u[:, :, :], tile_of(d["u"], i)).then_inc(u_loaded, 16)
                sp.dma_start(sz[:, :, :], tile_of(d["sz"], i)).then_inc(sz_loaded, 16)
                sp.wait_ge(x1_done, i + 1)
                sp.dma_start(res[:, :, :], d["res"].rearrange("(i s p) c -> i p s c", s=SUB, p=P)[i]
                             ).then_inc(res_loaded, 16)

            def store(i):
                sp.wait_ge(out_done, i + 3)
                sp.dma_start(d["out"].rearrange("(i s p) c -> i p s c", s=SUB, p=P)[i],
                             out[:, :, :]).then_inc(out_stored, 16)

            load(0)
            load(1)
            with sp.Fori(0, NT - 2) as i:
                load(i + 2)
                store(i)
            store(NT - 2)
            store(NT - 1)
            sp.wait_ge(out_stored, 16 * (NT + 1))

        @block.tensor
        def _(pe):
            pe.wait_ge(consts, 3)
            pe.sem_inc(tr_ready, 4)
            pe.sem_inc(gu_ready, MH)
            pe.sem_inc(proj_ready, 1)
            pe.sem_inc(down_ready, 1)
            pe.wait_ge(w_loaded, 64)
            pe.wait_ge(w_wide, 1)

            def first(i, s, k):
                if k == 0:
                    pe.wait_ge(y_loaded, i * 64 + 64)
                    for m in range(MI):
                        if m < 2:
                            pe.wait_ge(xrest_done, i * 2 + m + 1)
                        else:
                            pe.wait_ge(y_taken, i * 4 + m + 3)
                        for g in range(SUB):
                            last = nc.tensor.transpose(tr[:, m % 2, g * P:(g + 1) * P], y[:, g, m, :], ident[:, :])
                        last.then_inc(tr_ready, 1)
                if k == 1:
                    pe.wait_ge(gated, i * 4 + 8)
                    pe.wait_ge(out_done, i + 1)
                    pe.wait_ge(x1_done, i + 1)
                    for g in range(SUB):
                        for m in range(MI):
                            last = nc.tensor.matmul(ob[:, g, :], yg[:, m, g * P:(g + 1) * P], w_out[:, m, :],
                                                    start=(m == 0), stop=(m == MI - 1))
                    last.then_inc(proj_ready, 1)
                if k == 2:
                    pe.wait_ge(xf_done, i * 4 + 4)
                    pe.wait_ge(y_taken, i * 4 + 8)
                    for kk in range(KD):
                        for g in range(SUB):
                            last = nc.tensor.transpose(tr[:, kk, g * P:(g + 1) * P],
                                                       xf[:, g, kk * P:(kk + 1) * P], ident[:, :])
                        last.then_inc(tr_ready, 1)

            def second(i, s, k, last_tile=False):
                if k < 2:
                    if k == 0:
                        pe.wait_ge(xpart3, i * 2 + 2)
                    for m in range(3 * k, 3 * k + 3):
                        pe.wait_ge(hid_done, i * 6 + m + 5)
                        for r in range(2):
                            for n in range(3 * KD):
                                kk, part = n // 3, n % 3
                                last = nc.tensor.matmul(gu[:, m % 2, r, :], wgu[:, r, kk, m * P:(m + 1) * P],
                                                        xparts[:, part, kk, :], start=(n == 0),
                                                        stop=(n == 3 * KD - 1))
                        last.then_inc(gu_ready, 1)
                else:
                    pe.wait_ge(hid_done, i * 6 + 12)
                    pe.wait_ge(x1_done, NT + 1 if last_tile else i + 3)
                    for g in range(SUB):
                        for m in range(MH):
                            last = nc.tensor.matmul(ob[:, g, :], hid[:, m, g * P:(g + 1) * P], wd[:, m, :],
                                                    start=(m == 0), stop=(m == MH - 1))
                    last.then_inc(down_ready, 1)

            over_tiles(pe, first, second)

        @block.scalar
        def _(act):
            n_gu = 2 * KD * HID
            act.dma_start(wgu[:, :, :, :].rearrange("p w k h -> p (w k h)"),
                          d["w_turned"][:, 0:n_gu]).then_inc(w_loaded, 16)
            act.dma_start(wd_bf[:, :, :].rearrange("p m c -> p (m c)"), d["w_turned"][:, n_gu:]).then_inc(w_loaded, 16)
            act.dma_start(w_out[:, :, :], d["W_out"].rearrange("(m p) n -> p m n", p=P)).then_inc(w_loaded, 16)
            act.dma_start(dskip[:, :], d["D"].rearrange("(m p) -> p m", p=P),
                          allow_slow_non_contiguous=True).then_inc(w_loaded, 16)
            act.sem_inc(out_stored, 16)

            def first(i, s, k):
                if k != 2:
                    return
                act.wait_ge(gu_ready, i * MH + MH)
                for kk in range(KD):
                    act.wait_ge(tr_ready, i * 6 + 9 + kk)
                    nc.scalar.activation(xparts[:, 0, kk, :], tr[:, kk, :], ACT.Identity).then_inc(xpart1, 1)
                for kk in range(KD):
                    act.wait_ge(xrest_done, i * 2 + 3 + kk)
                    nc.scalar.activation(xparts[:, 1, kk, :], xrest[:, kk, :], ACT.Identity).then_inc(xpart2, 1)

            def second(i, s, k, last_tile=False):
                if k == 2:
                    return
                for m in range(3 * k, 3 * k + 3):
                    act.wait_ge(gu_ready, i * MH + MH + m + 1)
                    act.wait_ge(hid_done, i * MH + m + 5)
                    nc.scalar.activation(sg[:, m % 2, :], gu[:, m % 2, 0, :], ACT.Silu,
                                         scale=WSCALE).then_inc(silu_done, 1)

            over_tiles(act, first, second)

        @block.vector
        def _(dve):
            dve.wait_ge(w_loaded, 64)
            nc.vector.tensor_copy(wd[:, :, :], wd_bf[:, :, :]).then_inc(w_wide, 1)
            dve.sem_inc(xrest_done, 2)
            dve.sem_inc(y_taken, 4)
            dve.sem_inc(gated, 4)
            dve.sem_inc(x1_done, 1)
            dve.sem_inc(hid_done, MH)
            dve.sem_inc(out_done, 2)

            def first(i, s, k):
                if k == 0:
                    dve.wait_ge(u_loaded, i * 16 + 16)
                    dve.wait_ge(sz_loaded, i * 16 + 16)
                    dve.wait_ge(proj_ready, i + 1)
                    for m in range(MI):
                        dve.wait_ge(tr_ready, i * 6 + 5 + m)
                        nc.vector.scalar_tensor_tensor(out=yg[:, m, :], in0=u[:, m, :], scalar=dskip[:, m:m + 1],
                                                       in1=tr[:, m % 2, :], op0=ALU.mult,
                                                       op1=ALU.add).then_inc(y_taken, 1)
                    for m in range(MI):
                        dve.wait_ge(y_taken, i * 4 + 5 + m)
                        nc.vector.tensor_tensor(yg[:, m, :], yg[:, m, :], sz[:, m, :], ALU.mult).then_inc(gated, 1)
                if k == 1:
                    dve.wait_ge(res_loaded, i * 16 + 16)
                    dve.wait_ge(proj_ready, i + 2)
                    nc.vector.tensor_tensor(x1[:, s], ob[:, :, :], res[:, :, :], ALU.add).then_inc(x1_done, 1)
                    dve.wait_ge(x1_done, i + 2)
                    for g in range(SUB):
                        nc.vector.bn_stats(stats[:, g, :], x1[:, s, g, :]).then_inc(stats_done, 1)
                    dve.wait_ge(stats_done, i * 4 + 4)
                    nc.vector.memset(spare[:, 0:1], 0.0)
                    for g in range(SUB):
                        nc.vector.bn_aggr(mv[:, g, :], stats[:, g, :]).then_inc(mv_done, 1)
                    dve.wait_ge(mv_done, i * 4 + 4)
                    nc.vector.tensor_scalar(veps[:, :], mv[:, :, 1], EPS, None, ALU.add).then_inc(veps_done, 1)
                    dve.wait_ge(rstd_done, i + 1)
                    dve.wait_ge(tr_ready, i * 6 + 4)
                    for g in range(SUB):
                        nc.vector.tensor_scalar(xf[:, g, :], x1[:, s, g, :], mv[:, g, 0:1], rstd[:, g:g + 1],
                                                ALU.subtract, ALU.mult).then_inc(xf_done, 1)
                if k == 2:
                    for kk in range(KD):
                        dve.wait_ge(xpart1, i * 2 + 1 + kk)
                        nc.vector.tensor_tensor(xrest[:, kk, :], tr[:, kk, :], xparts[:, 0, kk, :],
                                                ALU.subtract).then_inc(xrest_done, 1)

            def second(i, s, k, last_tile=False):
                if k < 2:
                    if k == 0:
                        dve.wait_ge(down_ready, i + 1)
                    for m in range(3 * k, 3 * k + 3):
                        dve.wait_ge(silu_done, i * MH + m + 1)
                        nc.vector.scalar_tensor_tensor(out=hid[:, m, :], in0=gu[:, m % 2, 1, :], scalar=WSCALE,
                                                       in1=sg[:, m % 2, :], op0=ALU.mult,
                                                       op1=ALU.mult).then_inc(hid_done, 1)
                else:
                    dve.wait_ge(down_ready, i + 2)
                    dve.wait_ge(out_stored, i * 16 + 16)
                    nc.vector.scalar_tensor_tensor(out=out[:, :, :], in0=ob[:, :, :], scalar=WSCALE, in1=x1[:, s],
                                                   op0=ALU.mult, op1=ALU.add).then_inc(out_done, 1)

            over_tiles(dve, first, second)

        @block.gpsimd
        def _(pool):
            nc.gpsimd.memset(half[:, :], -0.5).then_inc(consts, 1)
            nc.gpsimd.memset(ident[:, :], 0.0).then_inc(consts, 1)
            pool.wait_ge(consts, 2)
            nc.gpsimd.affine_select(out=ident[:, :], in_=ident[:, :], compare_op=ALU.not_equal, fill=1.0, base=0,
                                    pattern=[[-1, P]], channel_multiplier=1).then_inc(consts, 1)
            with pool.Fori(0, NT) as i:
                pool.wait_ge(veps_done, i + 1)
                nc.gpsimd.tensor_tensor(rstd[:, :], veps[:, :], half[:, :], ALU.pow).then_inc(rstd_done, 1)
                for kk in range(KD):
                    pool.wait_ge(xpart2, i * 2 + 1 + kk)
                    nc.gpsimd.tensor_tensor(xparts[:, 2, kk, :], xrest[:, kk, :], xparts[:, 1, kk, :],
                                            ALU.subtract).then_inc(xpart3, 1)


def build(nc, d):
    d = dict(d)

    def scratch(name, shape, dt=F32):
        d[name] = nc.dram_tensor(f"scratch_{name}", shape, dt, kind="Internal").ap()

    scratch("res", [TOK, DM])
    scratch("u", [DI, TOK])
    scratch("sz", [DI, TOK])
    scratch("B", [P, TOK])
    scratch("C", [P, TOK])
    scratch("dparts", [3, DI, TOK], BF16)
    scratch("uparts", [3, DI, TOK], BF16)
    scratch("w_turned", [P, N_TURNS * P], BF16)
    scratch("a_parts", [3, DI, NS], BF16)
    scratch("a_image", [NG, P, PAIRS * P], BF16)
    scratch("y", [2 + NG * NB, 2 * CH, 64])
    with nc.sbuf_tensor("xnT", [P, KD, TOK], F32) as xnT:
        norm_stage(nc, d, xnT)
        project_stage(nc, d, xnT)
    scan_stage(nc, d)
    output_stage(nc, d)


_INS = ["x", "ln_w", "ln_b", "W_in", "conv_w", "conv_b", "W_xproj", "W_dt", "b_dt", "A_log", "D", "W_out"]
_FFN = ["w_gate", "w_up", "w_down"]


def kernel(**inputs):
    import numpy as np
    import concourse.bacc as bacc
    from concourse.bass_utils import run_bass_kernel_spmd

    nc = bacc.Bacc("TRN2", target_bir_lowering=False, num_devices=1, dynamic_dma_scratch_size=1024)
    arrays, d = {}, {}
    for name, key in [(n, f"L0_attn_{n}") for n in _INS] + [(n, f"L0_ffn_{n}") for n in _FFN]:
        a = np.ascontiguousarray(inputs[key])
        arrays[f"in_{name}"] = a
        d[name] = nc.dram_tensor(f"in_{name}", a.shape, mybir.dt.from_np(a.dtype), kind="ExternalInput").ap()
    d["x"] = d["x"].rearrange("b t c -> (b t) c")
    out = nc.dram_tensor("out", (BATCH, SEQ, DM), F32, kind="ExternalOutput").ap()
    d["out"] = out.rearrange("b t c -> (b t) c")
    build(nc, d)
    return run_bass_kernel_spmd(nc, [arrays], core_ids=[0]).results[0]["out"]
```
